# Optimizing a Trainium2 kernel written in Bass

```python
import numpy as np
import jax
import jax.numpy as jnp

def _softmax(x, axis=-1):
    return jax.nn.softmax(x, axis=axis)

def _gelu(x):
    return jax.nn.gelu(x, approximate=True)

def _silu(x):
    return jax.nn.silu(x)

def _sigmoid(x):
    return jax.nn.sigmoid(x)

def _layernorm(x, axis=-1, eps=1e-05):
    m = jnp.mean(x, axis=axis, keepdims=True)
    v = jnp.var(x, axis=axis, keepdims=True)
    return (x - m) / jnp.sqrt(v + eps)

def _scatter_add(tgt, idx, src, axis=0):
    return tgt.at[idx].add(src)

def _segment_sum(src, seg, n):
    return jax.ops.segment_sum(src, seg, n)
kernel_name = 'mk_flamingo_gated_d2_seqx_r8_6593bd'

def setup_inputs(seed: int=0):
    np.random.seed(seed)
    _w = jnp.asarray

    def _rec_inputs():
        import jax
        import jax.numpy as jnp
        _rk = jax.random.key(seed)
        x = -0.000125 + 0.9999 * jax.random.normal(jax.random.fold_in(_rk, 1), (8, 128, 256), jnp.float32)
        _lenS = 128 - jax.random.randint(jax.random.fold_in(_rk, 7), (8,), 0, max(1, 128 // 4) + 1, jnp.int32)
        _lenS2 = 128 - jax.random.randint(jax.random.fold_in(_rk, 8), (8,), 0, max(1, 128 // 4) + 1, jnp.int32)
        _ctx_2048P = jax.random.normal(jax.random.fold_in(_rk, 11), (8, 16, 256), jnp.float32)
        _ctx_2048c = jax.random.dirichlet(jax.random.fold_in(_rk, 511), 0.3 * jnp.ones((16,), jnp.float32), (8, 128))
        _ctx_2048t = jnp.einsum('bsk,bkd->bsd', _ctx_2048c, _ctx_2048P)
        _ctx_2048t = _ctx_2048t * jax.lax.rsqrt(jnp.mean(jnp.square(_ctx_2048t)) + 1e-12) * 0.953939
        ctx_2048 = -0.000514642 + 1.00011 * (_ctx_2048t + 0.3 * jax.random.normal(jax.random.fold_in(_rk, 611), (8, 128, 256), jnp.float32))
        _validS = jnp.arange(128)[None, :] < _lenS[:, None]
        _validS2 = jnp.arange(128)[None, :] < _lenS2[:, None]
        _causal = jnp.tril(jnp.ones((128, 128), dtype=bool))
        mask_BxS2_bk0 = jnp.logical_not(jnp.broadcast_to(_validS2[:, :], (8, 128)))
        _g = jax.random.normal(jax.random.fold_in(_rk, 9001), (2, 2), jnp.float32)
        _g = jnp.sign(_g) * jnp.maximum(jnp.abs(_g), 1.0) + (_g == 0) * 1.0
        g_xattn = _g[0]
        g_ffn = _g[1]
        return (x, ctx_2048, mask_BxS2_bk0, g_xattn, g_ffn)
    x, ctx_2048, mask_BxS2_bk0, g_xattn, g_ffn = _rec_inputs()

    def _L0_xattn_setup():
        import jax, jax.numpy as jnp
        import numpy as np
        key = jax.random.key(seed)
        k1, k2, k3 = jax.random.split(key, 3)
        B, S, D, M = (8, 256, 256, 128)
        hidden_states = jax.random.normal(k1, (B, S, D), dtype=jnp.float32)
        memory_tokens = jax.random.normal(k2, (B, M, D), dtype=jnp.float32)
        memory_mask = jax.random.randint(k3, (B, M), 0, 2).astype(jnp.bool_)
        return {'hidden_states': hidden_states, 'memory_tokens': memory_tokens, 'memory_mask': memory_mask}
    _L0_xattn_all = _L0_xattn_setup()
    _L0_xattn_in = {k: v for k, v in _L0_xattn_all.items() if k in ()}
    del _L0_xattn_all

    def _L0_ffn_setup():
        import jax, jax.numpy as jnp
        import numpy as np
        B, S, D, F, E, K = (2, 256, 256, 1024, 8, 2)
        key = jax.random.key(seed)
        k0, k1, k2, k3 = jax.random.split(key, 4)
        scale = lambda k, shape, fan_in: jax.random.normal(k, shape, jnp.float32) * fan_in ** (-0.5)
        return {'inputs': jax.random.normal(k0, (B, S, D), jnp.float32), 'gate_w': scale(k1, (D, E), D), 'gate_b': jnp.zeros((E,), jnp.float32), 'w1': scale(k2, (E, D, F), D), 'b1': jnp.zeros((E, F), jnp.float32), 'w2': scale(k3, (E, F, D), F), 'b2': jnp.zeros((E, D), jnp.float32)}
    _L0_ffn_all = _L0_ffn_setup()
    _L0_ffn_in = {k: v for k, v in _L0_ffn_all.items() if k in ('gate_w', 'gate_b', 'w1', 'b1', 'w2', 'b2')}
    del _L0_ffn_all

    def _L1_xattn_setup():
        import jax, jax.numpy as jnp
        import numpy as np
        from math import sqrt
        key = jax.random.key(seed)
        kq, kk, kv = jax.random.split(key, 3)
        B, D, N = (8, 128, 256)
        Q = jax.random.normal(kq, (B, D, N), dtype=jnp.float32)
        K = jax.random.normal(kk, (B, D, N), dtype=jnp.float32)
        V = jax.random.normal(kv, (B, D, N), dtype=jnp.float32)
        return {'Q': Q, 'K': K, 'V': V}
    _L1_xattn_all = _L1_xattn_setup()
    _L1_xattn_in = {k: v for k, v in _L1_xattn_all.items() if k in ()}
    del _L1_xattn_all

    def _L1_ffn_setup():
        import jax, jax.numpy as jnp
        import numpy as np
        B, S, H = (2, 64, 256)
        E, I, K = (64, 176, 6)
        NS = 2
        SH_I = I * NS
        key = jax.random.key(seed)
        ks = jax.random.split(key, 6)
        s = 0.02
        return {'hidden_states': jax.random.normal(ks[0], (B, S, H), jnp.float32), 'gate_w': jax.random.normal(ks[1], (E, H), jnp.float32) * s, 'experts_w1': jax.random.normal(ks[2], (E, I, H), jnp.float32) * s, 'experts_w2': jax.random.normal(ks[3], (E, H, I), jnp.float32) * s, 'shared_gate_up': jax.random.normal(ks[4], (2 * SH_I, H), jnp.float32) * s, 'shared_down': jax.random.normal(ks[5], (H, SH_I), jnp.float32) * s}
    _L1_ffn_all = _L1_ffn_setup()
    _L1_ffn_in = {k: v for k, v in _L1_ffn_all.items() if k in ('gate_w', 'experts_w1', 'experts_w2', 'shared_gate_up', 'shared_down')}
    del _L1_ffn_all
    return {'x': x, 'ctx_2048': ctx_2048, 'mask_BxS2_bk0': mask_BxS2_bk0, 'g_xattn': g_xattn, 'g_ffn': g_ffn, 'L0_ffn_gate_w': _L0_ffn_in['gate_w'], 'L0_ffn_gate_b': _L0_ffn_in['gate_b'], 'L0_ffn_w1': _L0_ffn_in['w1'], 'L0_ffn_b1': _L0_ffn_in['b1'], 'L0_ffn_w2': _L0_ffn_in['w2'], 'L0_ffn_b2': _L0_ffn_in['b2'], 'L1_ffn_gate_w': _L1_ffn_in['gate_w'], 'L1_ffn_experts_w1': _L1_ffn_in['experts_w1'], 'L1_ffn_experts_w2': _L1_ffn_in['experts_w2'], 'L1_ffn_shared_gate_up': _L1_ffn_in['shared_gate_up'], 'L1_ffn_shared_down': _L1_ffn_in['shared_down']}

def reference(x, ctx_2048, mask_BxS2_bk0, g_xattn, g_ffn, L0_ffn_gate_w, L0_ffn_gate_b, L0_ffn_w1, L0_ffn_b1, L0_ffn_w2, L0_ffn_b2, L1_ffn_gate_w, L1_ffn_experts_w1, L1_ffn_experts_w2, L1_ffn_shared_gate_up, L1_ffn_shared_down):
    import jax
    import jax.numpy as jnp

    def _L0_xattn_ref(hidden_states, memory_tokens, memory_mask):
        import jax, jax.numpy as jnp
        import numpy as np
        B, S, D = hidden_states.shape
        scale = 1.0 / jnp.sqrt(jnp.asarray(D, hidden_states.dtype))
        scores = jnp.einsum('bsd,bmd->bsm', hidden_states, memory_tokens) * scale
        neg_inf = jnp.asarray(-1e+30, scores.dtype)
        scores = jnp.where(memory_mask[:, None, :], scores, neg_inf)
        attn = jax.nn.softmax(scores, axis=-1)
        readout = jnp.einsum('bsm,bmd->bsd', attn, memory_tokens)
        valid_b = jnp.any(memory_mask, axis=-1)
        out = jnp.where(valid_b[:, None, None], readout, jnp.zeros_like(readout))
        return out

    def _L0_ffn_ref(inputs, gate_w, gate_b, w1, b1, w2, b2):
        import jax, jax.numpy as jnp
        import numpy as np
        B, S, D, F, E, K = (2, 256, 256, 1024, 8, 2)
        x = inputs.reshape(-1, inputs.shape[-1])
        n = x.shape[0]
        gate_probs = jax.nn.softmax(x @ gate_w + gate_b, axis=-1)
        weights, selected = jax.lax.top_k(gate_probs, K)
        weights = weights / jnp.sum(weights, axis=-1, keepdims=True)
        comb = jnp.zeros((n, E), x.dtype).at[jnp.arange(n)[:, None], selected].set(weights)
        h = jax.nn.gelu(jnp.einsum('nd,edf->enf', x, w1) + b1[:, None, :])
        expert_out = jnp.einsum('enf,efd->end', h, w2) + b2[:, None, :]
        out = jnp.einsum('ne,end->nd', comb, expert_out)
        return out.reshape(inputs.shape[:-1] + (out.shape[-1],))

    def _L1_xattn_ref(Q, K, V):
        import jax, jax.numpy as jnp
        import numpy as np
        from math import sqrt
        dk = Q.shape[1]
        x = jnp.einsum('bdn,bdm->bnm', Q, K) / sqrt(dk)
        score = jax.nn.sigmoid(x)
        out = jnp.einsum('bvn,bnm->bvm', V, score)
        return out

    def _L1_ffn_ref(hidden_states, gate_w, experts_w1, experts_w2, shared_gate_up, shared_down):
        import jax, jax.numpy as jnp
        import numpy as np
        B, S, H = (2, 64, 256)
        E, I, K = (64, 176, 6)
        NS = 2
        SH_I = I * NS
        orig_shape = hidden_states.shape
        x = hidden_states.reshape(-1, orig_shape[-1])
        router_logits = x @ gate_w.T
        probs = jax.nn.softmax(router_logits, axis=-1)
        topk_w, topk_idx = jax.lax.top_k(probs, K)
        topk_w = topk_w / jnp.sum(topk_w, axis=-1, keepdims=True)
        combine = jnp.sum(jax.nn.one_hot(topk_idx, E, dtype=x.dtype) * topk_w[..., None], axis=1)
        h = jax.nn.silu(jnp.einsum('th,eih->tei', x, experts_w1))
        y = jnp.einsum('tei,ehi->teh', h, experts_w2)
        routed_out = jnp.einsum('teh,te->th', y, combine)
        gu = x @ shared_gate_up.T
        g, u = jnp.split(gu, 2, axis=-1)
        shared_out = jax.nn.silu(g) * u @ shared_down.T
        return (routed_out + shared_out).reshape(orig_shape)
    x = x + jnp.tanh(g_xattn[0]) * _L0_xattn_ref(_layernorm(x, axis=-1), ctx_2048, mask_BxS2_bk0)
    x = x + jnp.tanh(g_ffn[0]) * _L0_ffn_ref(_layernorm(x, axis=-1), L0_ffn_gate_w, L0_ffn_gate_b, L0_ffn_w1, L0_ffn_b1, L0_ffn_w2, L0_ffn_b2)
    x = x + jnp.tanh(g_xattn[1]) * _L1_xattn_ref(_layernorm(x, axis=-1), ctx_2048, ctx_2048)
    x = x + jnp.tanh(g_ffn[1]) * _L1_ffn_ref(_layernorm(x, axis=-1), L1_ffn_gate_w, L1_ffn_experts_w1, L1_ffn_experts_w2, L1_ffn_shared_gate_up, L1_ffn_shared_down)
    return x

_drawn_inputs = setup_inputs


def setup_inputs(seed=0):
    import zlib

    import numpy as np

    out = dict(_drawn_inputs(seed))
    spreads = {'g_ffn': (-1.0, 0.6),
     'L0_ffn_gate_b': (0.0, 0.71),
     'L0_ffn_b1': (0.0, 0.8),
     'L0_ffn_b2': (0.0, 0.684)}
    factors = {'L1_ffn_gate_w': 8.0,
     'L1_ffn_experts_w1': 8.0,
     'L1_ffn_experts_w2': 8.0,
     'L1_ffn_shared_gate_up': 8.0,
     'L1_ffn_shared_down': 8.0}
    for name, (base, spread) in spreads.items():
        noise = np.random.default_rng([zlib.crc32(name.encode()), seed]).standard_normal(out[name].shape)
        drawn = base * np.exp(spread * noise) if base else spread * noise
        out[name] = jnp.asarray(drawn.astype(out[name].dtype))
    for name, factor in factors.items():
        out[name] = (out[name] * factor).astype(out[name].dtype)
    return out
```

```python
import concourse.bass as bass
from concourse import mybir
from contextlib import ExitStack

F32 = mybir.dt.float32
F32R = mybir.dt.float32r
U8 = mybir.dt.uint8
ALU = mybir.AluOpType
ACT = mybir.ActivationFunctionType
AX_X = mybir.AxisListType.X

P = 128
B, S, D = 8, 128, 256
KD = D // P
TOK = B * S
HALF = TOK // 2
PAIRS = B // 2

E0, F0, TOP0 = 8, 1024, 2
E1, I1, TOP1, SH1 = 64, 176, 6, 352
EPS = 1e-5
NEG = -1e30

ROUNDS = 8
CH0 = F0 // P
EPR0 = E0 // ROUNDS
EPR1 = E1 // ROUNDS
CH1 = EPR1 * I1 // P
SHC = -(-SH1 // P)
SLOTS = CH1
STEPS0, STEPSH, STEPS1 = 2 * CH0 * ROUNDS, 2 * SHC, 2 * CH1 * ROUNDS
BASE_SH = STEPS0
BASE1 = STEPS0 + STEPSH
LAST = STEPS0 + STEPSH + STEPS1
WB_SH = CH0 * ROUNDS
WB1 = WB_SH + 2 * SHC
CREDIT = 2


def loads_before(layer, slot):
    if layer == 0:
        return 0
    return (ROUNDS if slot < CH0 else 0) + (1 if slot < 2 * SHC else 0)


def flamingo_kernel(nc, x, ctx, ctx_t, mask, g_xattn, g_ffn, gate0, gate0_b, w0, b1, b2,
                    gate1, w1, w_shared, sel_rows, out):
    comb_rows = nc.dram_tensor("comb_rows", (2, 2, E1, TOK), F32).ap()

    with ExitStack() as stack:
        def sb(name, shape, dt=F32):
            return stack.enter_context(nc.sbuf_tensor(name, shape, dt))

        def sem(name):
            return stack.enter_context(nc.semaphore(name))

        xs = sb("xs", [P, B, D])
        xn = sb("xn", [P, B, D])
        xn_t = sb("xn_t", [P, KD, TOK])
        xt_hi = sb("xt_hi", [P, KD, TOK], F32R)
        xt_lo = sb("xt_lo", [P, KD, TOK], F32R)
        ctx_sb = sb("ctx_sb", [P, B, D])
        ctx_tsb = sb("ctx_tsb", [P, B, KD, S])
        mask_sb = sb("mask_sb", [P, B, S], U8)
        ident = sb("ident", [P, P])
        gains = sb("gains", [P, 4])
        tanh_g = sb("tanh_g", [P, 4])
        valid_u8 = sb("valid_u8", [P, B])
        row_max = sb("row_max", [P, B])
        neg_max = sb("neg_max", [P, B])
        row_sum = sb("row_sum", [P, B])
        row_inv = sb("row_inv", [P, B])
        row_gain = sb("row_gain", [P, B])
        stats = sb("stats", [P, B, 6])
        mean_var = sb("mean_var", [P, B, 2])
        std = sb("std", [P, B])
        rstd = sb("rstd", [P, B])
        gate_sb = [sb("gate0_sb", [P, KD, E0]), sb("gate1_sb", [P, KD, E1])]
        gate_b_sb = sb("gate_b_sb", [P, E0])
        b1_sb = sb("b1_sb", [P, WB_SH])
        b1_round = sb("b1_round", [P, CH0])
        b2_sb = sb("b2_sb", [E0, D])
        sel_f = sb("sel_f", [2 * EPR1, CH1, P])
        sel = sb("sel", [2 * EPR1, CH1, P], F32R)
        ones_f = sb("ones_f", [2, P])
        ones2 = sb("ones2", [2, P], F32R)
        stage = sb("stage", [P, SLOTS, 2 * D])
        w_hi = sb("w_hi", [P, SLOTS, 2 * D], F32R)
        w_lo = sb("w_lo", [P, SLOTS, 2 * D], F32R)
        act_out = sb("act_out", [P, 2, HALF])
        hid = sb("hid", [P, 2, HALF])
        hid_hi = sb("hid_hi", [P, 2, HALF], F32R)
        hid_lo = sb("hid_lo", [P, 2, HALF], F32R)
        y_t = sb("y_t", [P, KD, TOK])
        masked = y_t[:, 0, :].rearrange("p (b s) -> p b s", b=B)
        probs = y_t[:, 1, :].rearrange("p (b s) -> p b s", b=B)
        probs_t = hid[:].rearrange("p h (b s) -> p (h b) s", s=S)
        score1 = act_out
        logit = sb("logit", [P, B * E1])
        expo = sb("expo", [P, B * E1])
        pext = [sb("pext0", [P, B, E0 + 8 - TOP0]), sb("pext1", [P, B, E1 + 8 - TOP1])]
        prep = [sb("prep0", [P, B, E0 + 8 - TOP0]), sb("prep1", [P, B, E1 + 8 - TOP1])]
        top8 = sb("top8", [P, B, 8])
        comb = sb("comb", [P, B, E1])
        comb_t = sb("comb_t", [E0, TOK])
        comb_hi = sb("comb_hi", [E1, TOK], F32R)
        comb_lo = sb("comb_lo", [E1, TOK], F32R)
        comb_next = sb("comb_next", [2 * EPR1, TOK])
        comb_cur = sb("comb_cur", [2 * EPR1, TOK], F32R)
        zero = sb("zero", [P, 1])
        scratch = sb("scratch", [P, 4])

        ps_h = [stack.enter_context(nc.psum_tensor(f"ps_h{i}", [P, HALF], F32)) for i in range(2)]
        ps_c = [stack.enter_context(nc.psum_tensor(f"ps_c{i}", [P, HALF], F32)) for i in range(2)]
        ps_o = [stack.enter_context(nc.psum_tensor(f"ps_o{i}", [P, HALF], F32)) for i in range(4)]
        ps_t = ps_h + ps_c

        x_in, ctx_in, ctx_t_in, small_in, sel_in = (sem(n) for n in ("x_in", "ctx_in", "ctx_t_in", "small_in", "sel_in"))
        const_ready = sem("const_ready")
        vec = sem("vec")
        gains_ready, var_ready, std_ready, xn_ready = (sem(n) for n in ("gains_ready", "var_ready", "std_ready", "xn_ready"))
        xn_turned, xn_t_ready, xt_hi_ready, xt_lo_ready = (sem(n) for n in ("xn_turned", "xn_t_ready", "xt_hi_ready", "xt_lo_ready"))
        score0_ready, max_ready, probs_ready, probs_turned, probs_t_ready, read0_ready = (
            sem(n) for n in ("score0_ready", "max_ready", "probs_ready", "probs_turned", "probs_t_ready", "read0_ready"))
        score1_done, score1_ready, read1_ready, read1_used = (sem(n) for n in ("score1_done", "score1_ready", "read1_ready", "read1_used"))
        logits_done, shifted_ready, expo_ready, comb_ready, comb_turned, comb_t_ready, comb_split, comb_out = (
            sem(n) for n in ("logits_done", "shifted_ready", "expo_ready", "comb_ready", "comb_turned", "comb_t_ready", "comb_split", "comb_out"))
        w_in = [sem(f"w_in{t}") for t in range(SLOTS)]
        w_split, comb_in, comb_copied = sem("w_split"), sem("comb_in"), sem("comb_copied")
        up_done, sel_done, act_done, mult_done, hi_done, lo_done, down_done = (
            sem(n) for n in ("up_done", "sel_done", "act_done", "mult_done", "hi_done", "lo_done", "down_done"))
        y_ready_act, y_ready_dve, y_turned, out_ready, stored = (
            sem(n) for n in ("y_ready_act", "y_ready_dve", "y_turned", "out_ready", "stored"))
        split_hi, bias_ready = sem("split_hi"), sem("bias_ready")

        block = stack.enter_context(nc.Block())

        @block.sync
        def _(sp):
            for q in range(4):
                sp.dma_start(xs[:, 2 * q:2 * q + 2, :], x[2 * q:2 * q + 2].rearrange("b s d -> s b d")).then_inc(x_in, 16)
            sp.dma_start(ctx_tsb[:], ctx_t).then_inc(ctx_t_in, 16)
            sp.dma_start(ctx_sb[:], ctx.rearrange("b s d -> s b d")).then_inc(ctx_in, 16)
            for dst, src in ((gate_sb[0][:], gate0), (gate_sb[1][:], gate1), (gate_b_sb[:], gate0_b.partition_broadcast(P)),
                             (b1_sb[:], b1), (b2_sb[:], b2)):
                sp.dma_start(dst, src).then_inc(small_in, 16)
            sp.dma_start(sel_f[:], sel_rows).then_inc(sel_in, 16)

            def load_weights(source, layer, i, t, block_no):
                if block_no is not None:
                    sp.wait_ge(w_split, block_no + 1)
                sp.dma_start(stage[:, t, :], source[i, t]).then_inc(w_in[t], 16)

            def load_comb(layer, n, source_round, epr):
                if n is not None:
                    sp.wait_ge(comb_copied, n)
                for half in range(2):
                    sp.dma_start(comb_next[half * epr:(half + 1) * epr, :],
                                 comb_rows[layer, half].rearrange("(r e) t -> r e t", e=epr)[source_round]
                                 ).then_inc(comb_in, 16)

            w0_v = w0.rearrange("(i t) p n -> i t p n", t=CH0)
            w1_v = w1.rearrange("(i t) p n -> i t p n", t=CH1)
            for t in range(CH0):
                load_weights(w0_v, 0, 0, t, None)
            sp.wait_ge(comb_out, 32)
            load_comb(0, None, 0, EPR0)
            with sp.Fori(1, ROUNDS) as i:
                for t in range(CH0):
                    load_weights(w0_v, 0, i, t, (i - 1) * CH0 + t)
                    if t == 0:
                        load_comb(0, i, i, EPR0)
            for j in range(2 * SHC):
                sp.wait_ge(w_split, (ROUNDS - 1) * CH0 + j + 1)
                sp.dma_start(stage[:, j, :], w_shared[j]).then_inc(w_in[j], 16)
            for t in list(range(2 * SHC, CH1)) + list(range(2 * SHC)):
                before = WB_SH + t if t < 2 * SHC else ((ROUNDS - 1) * CH0 + t if t < CH0 else None)
                load_weights(w1_v, 1, 0, t, before)
            sp.wait_ge(comb_out, 64)
            load_comb(1, ROUNDS, 0, EPR1)
            with sp.Fori(1, ROUNDS) as i:
                for t in range(CH1):
                    load_weights(w1_v, 1, i, t, (i - 1) * CH1 + t + WB1)
                    if t == 0:
                        load_comb(1, i + ROUNDS, i, EPR1)
            for q in range(PAIRS):
                sp.wait_ge(out_ready, PAIRS + q + 1)
                sp.dma_start(out[2 * q:2 * q + 2].rearrange("b s d -> s b d"), xs[:, 2 * q:2 * q + 2, :]).then_inc(stored, 16)
            sp.wait_ge(stored, 16 * PAIRS)

        @block.gpsimd
        def _(pool):
            pool.memset(zero[:], 0.0).then_inc(const_ready, 1)
            pool.memset(ident[:], 0.0).then_inc(const_ready, 1)
            pool.wait_ge(const_ready, 2)
            pool.affine_select(out=ident[:], in_=ident[:], compare_op=ALU.not_equal, fill=1.0, base=0,
                               pattern=[[-1, P]], channel_multiplier=1).then_inc(const_ready, 1)
            pool.memset(scratch[:, 0:1], 0.0).then_inc(act_done, CREDIT)
            pool.memset(scratch[:, 1:2], 0.0).then_inc(mult_done, CREDIT)
            pool.memset(scratch[:, 2:3], 0.0).then_inc(down_done, CREDIT)
            pool.memset(scratch[:, 3:4], 0.0).then_inc(lo_done, CREDIT)

            def split(t, loads, block_no, free_after):
                pool.wait_ge(w_in[t], 16 * loads)
                if free_after is not None:
                    pool.wait_ge(down_done, free_after)
                pool.tensor_tensor(w_hi[:, t, :], stage[:, t, :], zero[:].broadcast_to([P, 2 * D]), ALU.add).then_inc(split_hi, 1)
                pool.wait_ge(split_hi, block_no + 1)
                pool.tensor_tensor(w_lo[:, t, :], stage[:, t, :], w_hi[:, t, :].bitcast(F32), ALU.subtract
                                   ).then_inc(w_split, 1)

            def after_step(step):
                return step + 1 + CREDIT

            for t in range(CH0):
                split(t, 1, t, None)
            with pool.Fori(1, ROUNDS) as i:
                for t in range(CH0):
                    split(t, i + 1, i * CH0 + t, (i - 1) * (2 * CH0) + after_step(2 * t + 1))
            for j in range(2 * SHC):
                split(j, ROUNDS + 1, WB_SH + j, after_step(2 * ((ROUNDS - 1) * CH0 + j) + 1))
            for n, t in enumerate(range(CH1)):
                if t < 2 * SHC:
                    free = after_step(BASE_SH + 2 * (t % SHC) + 1)
                elif t < CH0:
                    free = after_step(2 * ((ROUNDS - 1) * CH0 + t) + 1)
                else:
                    free = None
                split(t, loads_before(1, t) + 1, WB1 + t, free)
            with pool.Fori(1, ROUNDS) as i:
                for t in range(CH1):
                    split(t, i + (loads_before(1, t) + 1), i * CH1 + (WB1 + t),
                          (i - 1) * (2 * CH1) + after_step(BASE1 + 2 * t + 1))

        @block.tensor
        def _(pe):
            def turn_norm(n):
                for q in range(PAIRS):
                    for b in (2 * q, 2 * q + 1):
                        pe.wait_ge(xn_ready, (0, 1, 3)[n] * B + b + 1)
                        for k in range(KD):
                            m = nc.tensor.transpose(ps_t[q][:, k * 2 * S + (b % 2) * S:k * 2 * S + (b % 2 + 1) * S],
                                                    xn[:, b, k * P:(k + 1) * P], ident[:])
                    m.then_inc(xn_turned, 1)

            def three(dst, w, w_cols, moving, m_cols, start, stop):
                (hi_w, lo_w), (hi_m, lo_m) = w, moving
                nc.tensor.matmul(dst, w_cols(hi_w), m_cols(hi_m), start=start, stop=False)
                nc.tensor.matmul(dst, w_cols(hi_w), m_cols(lo_m), start=False, stop=False)
                return nc.tensor.matmul(dst, w_cols(lo_w), m_cols(hi_m), start=False, stop=stop)

            def up(dst, t, half, first_col):
                for k in range(KD):
                    m = three(dst, (w_hi, w_lo), lambda w: w[:, t, first_col + k * P:first_col + (k + 1) * P],
                              (xt_hi, xt_lo), lambda v: v[:, k, half * HALF:(half + 1) * HALF], k == 0, k == KD - 1)
                return m

            def down(t, half, start, stop):
                for d in range(KD):
                    m = three(ps_o[2 * d + half][:], (w_hi, w_lo), lambda w: w[:, t, D + d * P:D + (d + 1) * P],
                              (hid_hi, hid_lo), lambda v: v[:, half, :], start, stop)
                m.then_inc(down_done, 1)

            def up_step(half, t, step, block_no):
                if half == 0:
                    pe.wait_ge(w_split, block_no + 1)
                pe.wait_ge(act_done, step + 1)
                up(ps_h[half][:], t, half, 0).then_inc(up_done, 1)

            def select(half, lhs, rounds_copied, rows):
                pe.wait_ge(comb_copied, rounds_copied)
                nc.tensor.matmul(ps_c[half][:], lhs, comb_cur[0:rows, half * HALF:(half + 1) * HALF],
                                 start=True, stop=True).then_inc(sel_done, 1)

            def round_steps(layer, i, last):
                chunks = CH0 if layer == 0 else CH1
                base = 0 if layer == 0 else BASE1
                wbase = 0 if layer == 0 else WB1
                steps = 2 * chunks
                for s in range(steps):
                    ahead = s + 2
                    wrap = ahead >= steps
                    t, half = (ahead % steps) // 2, s % 2
                    if not (last and wrap):
                        up_step(half, t, i * steps + (base + ahead), i * chunks + (wbase + ahead // 2))
                    pe.wait_ge(lo_done, i * steps + (base + s + 1 + CREDIT))
                    down(s // 2, half, False, last and s >= steps - 2)
                    if last and wrap:
                        continue
                    if layer == 1:
                        select(half, sel[:, t, :], i + (ROUNDS + 1 + (1 if wrap else 0)), 2 * EPR1)
                    elif t == 0:
                        select(half, ones2[:], i + 2, 2 * EPR0)

            def rounds(layer):
                base, wbase = (0, 0) if layer == 0 else (BASE1, WB1)
                for half in range(2):
                    up_step(half, 0, base + half, wbase)
                    if layer == 0:
                        select(half, ones2[:], 1, 2 * EPR0)
                    else:
                        select(half, sel[:, 0, :], ROUNDS + 1, 2 * EPR1)
                with pe.Fori(0, ROUNDS - 1) as i:
                    round_steps(layer, i, False)
                round_steps(layer, ROUNDS - 1, True)

            def router(layer):
                experts = (E0, E1)[layer]
                for b in range(B):
                    pe.wait_ge(xn_t_ready, PAIRS * (layer + 1) + b // 2 + 1)
                    for k in range(KD):
                        m = nc.tensor.matmul(ps_o[0][:, b * experts:(b + 1) * experts],
                                             xn_t[:, k, b * S:(b + 1) * S], gate_sb[layer][:, k, :],
                                             start=(k == 0), stop=(k == KD - 1))
                m.then_inc(logits_done, 1)
                pe.wait_ge(comb_ready, layer + 1)
                for b in range(B):
                    m = nc.tensor.transpose(ps_o[1 + b // 4][0:experts, (b % 4) * S:(b % 4 + 1) * S],
                                            comb[:, b, 0:experts], ident[:])
                m.then_inc(comb_turned, 1)

            def read1(b):
                pe.wait_ge(score1_ready, b + 1)
                for k in range(KD):
                    m = nc.tensor.matmul(ps_o[b // 2][:, (b % 2) * D:(b % 2 + 1) * D], ctx_tsb[:, b, k, :],
                                         score1[:, b % 2, k * D:(k + 1) * D], start=(k == 0), stop=(k == KD - 1))
                m.then_inc(read1_ready, 1)

            def turn_output(layer):
                pe.wait_ge(y_ready_act, 2 * (layer + 1))
                pe.wait_ge(y_ready_dve, 2 * (layer + 1))
                for b in range(B):
                    for d in range(KD):
                        m = nc.tensor.transpose(ps_t[b // 2][:, (b % 2) * D + d * P:(b % 2) * D + (d + 1) * P],
                                                y_t[:, d, b * S:(b + 1) * S], ident[:])
                    if b % 2:
                        m.then_inc(y_turned, 1)

            pe.wait_ge(const_ready, 3)
            turn_norm(0)
            pe.wait_ge(ctx_t_in, 16)
            for b in range(B):
                pe.wait_ge(xn_t_ready, b // 2 + 1)
                for k in range(KD):
                    m = nc.tensor.matmul(ps_o[b // 4][:, (b % 4) * S:(b % 4 + 1) * S], xn_t[:, k, b * S:(b + 1) * S],
                                         ctx_tsb[:, b, k, :], start=(k == 0), stop=(k == KD - 1))
                if b % 4 == 3:
                    m.then_inc(score0_ready, 1)
            for b in range(B):
                pe.wait_ge(probs_ready, b + 1)
                m = nc.tensor.transpose(ps_o[2 + b // 4][:, (b % 4) * S:(b % 4 + 1) * S], probs[:, b, :], ident[:])
                if b % 4 == 3:
                    m.then_inc(probs_turned, 1)
            pe.wait_ge(ctx_in, 16)
            for b in range(B):
                pe.wait_ge(probs_t_ready, b // 4 + 1)
                nc.tensor.matmul(ps_t[b // 2][:, (b % 2) * D:(b % 2 + 1) * D], probs_t[:, b, :], ctx_sb[:, b, :],
                                 start=True, stop=True).then_inc(read0_ready, 1)
            turn_norm(1)
            router(0)
            pe.wait_ge(comb_t_ready, 2)
            pe.wait_ge(comb_split, 1)
            for d in range(KD):
                for half in range(2):
                    nc.tensor.matmul(ps_o[2 * d + half][:], b2_sb[:, d * P:(d + 1) * P],
                                     comb_t[:, half * HALF:(half + 1) * HALF], start=True, stop=False)
            pe.wait_ge(xt_hi_ready, PAIRS)
            pe.wait_ge(xt_lo_ready, PAIRS)
            rounds(0)
            turn_output(0)
            for b in range(B):
                pe.wait_ge(xn_ready, 2 * B + b + 1)
                if b >= 4:
                    pe.wait_ge(score1_ready, b - 3)
                for k in range(KD):
                    m = nc.tensor.matmul(ps_t[b % 4][:, k * D:(k + 1) * D], xn[:, b, k * P:(k + 1) * P],
                                         ctx_sb[:, b, :], start=True, stop=True)
                m.then_inc(score1_done, 1)
                if b >= 1:
                    read1(b - 1)
            read1(B - 1)
            turn_norm(2)
            router(1)
            pe.wait_ge(comb_split, 2)
            pe.wait_ge(xt_hi_ready, 2 * PAIRS)
            pe.wait_ge(xt_lo_ready, 2 * PAIRS)
            for s in range(STEPSH + 2):
                if s < STEPSH:
                    up_step(s % 2, s // 2, BASE_SH + s, WB_SH + SHC + s // 2)
                if s >= 2:
                    pe.wait_ge(lo_done, BASE_SH + s - 1 + CREDIT)
                    down((s - 2) // 2, s % 2, s < 4, False)
                if s < STEPSH:
                    up(ps_c[s % 2][:], SHC + s // 2, s % 2, 0).then_inc(sel_done, 1)
            rounds(1)
            turn_output(1)

        @block.scalar
        def _(act):
            def root(n):
                act.wait_ge(var_ready, n + 1)
                nc.scalar.activation(std[:], mean_var[:, :, 1], ACT.Sqrt).then_inc(std_ready, 1)

            def take_turned(n):
                for q in range(PAIRS):
                    act.wait_ge(xn_turned, PAIRS * n + q + 1)
                    nc.scalar.activation(xn_t[:, :, q * 2 * S:(q + 1) * 2 * S],
                                         ps_t[q][:].rearrange("p (k t) -> p k t", k=KD), ACT.Copy).then_inc(xn_t_ready, 1)
                    if n > 0:
                        act.wait_ge(xn_t_ready, PAIRS * n + q + 1)
                        nc.scalar.activation(xt_hi[:, :, q * 2 * S:(q + 1) * 2 * S],
                                             xn_t[:, :, q * 2 * S:(q + 1) * 2 * S], ACT.Copy).then_inc(xt_hi_ready, 1)

            def router(layer):
                act.wait_ge(shifted_ready, layer + 1)
                n = B * (E0, E1)[layer]
                nc.scalar.activation(expo[:, 0:n], logit[:, 0:n], ACT.Exp).then_inc(expo_ready, 1)
                act.wait_ge(comb_split, layer + 1)
                for half, rows in enumerate((comb_hi, comb_lo)):
                    act.dma_start(comb_rows[layer, half, 0:(E0, E1)[layer], :], rows[0:(E0, E1)[layer], :].bitcast(F32)
                                  ).then_inc(comb_out, 16)

            def step(half, step_no, func, bias):
                act.wait_ge(up_done, step_no + 1)
                act.wait_ge(mult_done, step_no + 1)
                nc.scalar.activation(act_out[:, half, :], ps_h[half][:], func, bias=bias).then_inc(act_done, 1)
                act.wait_ge(mult_done, step_no + 1 + CREDIT)
                act.wait_ge(down_done, step_no + 1)
                nc.scalar.activation(hid_hi[:, half, :], hid[:, half, :], ACT.Copy).then_inc(hi_done, 1)

            def outputs(layer):
                for half in range(2):
                    act.wait_ge(down_done, (STEPS0, LAST)[layer] + CREDIT)
                    nc.scalar.activation(y_t[:, 0, half * HALF:(half + 1) * HALF], ps_o[half][:], ACT.Copy,
                                         scale=tanh_g[:, 2 + layer:3 + layer]).then_inc(y_ready_act, 1)

            act.dma_start(mask_sb[:], mask.partition_broadcast(P)).then_inc(small_in, 16)
            act.dma_start(gains[:, 0:2], g_xattn.partition_broadcast(P)).then_inc(small_in, 16)
            act.dma_start(gains[:, 2:4], g_ffn.partition_broadcast(P)).then_inc(small_in, 16)
            root(0)
            act.wait_ge(small_in, 16 * 8)
            nc.scalar.activation(tanh_g[:], gains[:], ACT.Tanh).then_inc(gains_ready, 1)
            take_turned(0)
            for b in range(B):
                act.wait_ge(max_ready, b // 4 + 1)
                nc.scalar.activation(probs[:, b, :], masked[:, b, :], ACT.Exp, bias=neg_max[:, b:b + 1],
                                     scale=float(D) ** -0.5, accum_out=row_sum[:, b:b + 1]).then_inc(probs_ready, 1)
            for g in range(2):
                act.wait_ge(probs_turned, g + 1)
                nc.scalar.activation(probs_t[:, 4 * g:4 * g + 4, :].rearrange("p b s -> p (b s)"), ps_o[2 + g][:],
                                     ACT.Copy).then_inc(probs_t_ready, 1)
            root(1)
            take_turned(1)
            router(0)
            for g in range(2):
                nc.scalar.activation(comb_t[:, g * HALF:(g + 1) * HALF], ps_o[1 + g][0:E0, :], ACT.Copy
                                     ).then_inc(comb_t_ready, 1)
            with act.Fori(0, ROUNDS) as i:
                nc.scalar.activation(b1_round[:], b1_sb[:, bass.ds(i * CH0, CH0)], ACT.Copy).then_inc(bias_ready, 1)
                act.wait_ge(bias_ready, i + 1)
                for s in range(2 * CH0):
                    step(s % 2, i * (2 * CH0) + s, ACT.Gelu_apprx_tanh, b1_round[:, s // 2:s // 2 + 1])
            outputs(0)
            root(2)
            for b in range(B):
                act.wait_ge(score1_done, b + 1)
                if b >= 2:
                    act.wait_ge(read1_ready, b - 1)
                nc.scalar.activation(score1[:, b % 2, :], ps_t[b % 4][:], ACT.Sigmoid, scale=float(S) ** -0.5
                                     ).then_inc(score1_ready, 1)
            root(3)
            take_turned(2)
            router(1)
            for s in range(STEPSH):
                step(s % 2, BASE_SH + s, ACT.Silu, 0.0)
            with act.Fori(0, ROUNDS) as i:
                for s in range(2 * CH1):
                    step(s % 2, i * (2 * CH1) + (BASE1 + s), ACT.Silu, 0.0)
            outputs(1)

        @block.vector
        def _(dve):
            count = [0]

            def link(ins):
                count[0] += 1
                ins.then_inc(vec, 1)
                dve.wait_ge(vec, count[0])

            def layernorm(n):
                for b in range(B):
                    if n == 0 and b % 2 == 0:
                        dve.wait_ge(x_in, 16 * PAIRS)
                    m = nc.vector.bn_stats(stats[:, b, :], xs[:, b, :])
                link(m)
                for b in range(B):
                    m = nc.vector.bn_aggr(mean_var[:, b, :], stats[:, b, :])
                link(m)
                nc.vector.tensor_scalar(mean_var[:, :, 1], mean_var[:, :, 1], EPS, None, ALU.add).then_inc(var_ready, 1)
                dve.wait_ge(std_ready, n + 1)
                link(nc.vector.reciprocal(rstd[:], std[:]))
                for b in range(B):
                    nc.vector.tensor_scalar(xn[:, b, :], xs[:, b, :], mean_var[:, b, 0:1], rstd[:, b:b + 1],
                                            ALU.subtract, ALU.mult).then_inc(xn_ready, 1)
                dve.wait_ge(xn_ready, B * (n + 1))

            def lower_half(n):
                for q in range(PAIRS):
                    dve.wait_ge(xt_hi_ready, PAIRS * n + q + 1)
                    cols = slice(q * 2 * S, (q + 1) * 2 * S)
                    nc.vector.tensor_tensor(xt_lo[:, :, cols], xn_t[:, :, cols], xt_hi[:, :, cols].bitcast(F32),
                                            ALU.subtract).then_inc(xt_lo_ready, 1)
                dve.wait_ge(xt_lo_ready, PAIRS * (n + 1))

            def over(v, n):
                return v.unsqueeze(2).broadcast_to([P, B, n])

            def router(layer):
                experts, top = ((E0, TOP0), (E1, TOP1))[layer]
                lg = logit[:, 0:B * experts].rearrange("p (b e) -> p b e", b=B)
                ex = expo[:, 0:B * experts].rearrange("p (b e) -> p b e", b=B)
                raw = ps_o[0][:, 0:B * experts].rearrange("p (b e) -> p b e", b=B)
                pe_, pr = pext[layer], prep[layer]
                dve.wait_ge(logits_done, layer + 1)
                if layer == 0:
                    link(nc.vector.tensor_tensor(lg, raw, gate_b_sb[:].unsqueeze(1).broadcast_to([P, B, E0]), ALU.add))
                else:
                    link(nc.vector.tensor_copy(lg, raw))
                link(nc.vector.tensor_reduce(row_max[:], lg, AX_X, ALU.max))
                nc.vector.tensor_tensor(lg, lg, over(row_max[:], experts), ALU.subtract).then_inc(shifted_ready, 1)
                dve.wait_ge(expo_ready, layer + 1)
                link(nc.vector.tensor_reduce(row_sum[:], ex, AX_X, ALU.add))
                link(nc.vector.reciprocal(row_inv[:], row_sum[:]))
                link(nc.vector.tensor_tensor(pe_[:, :, 0:experts], ex, over(row_inv[:], experts), ALU.mult))
                for b in range(B):
                    m = nc.vector.max(top8[:, b, :], pe_[:, b, 0:experts])
                link(m)
                link(nc.vector.memset(top8[:, :, top:8], -1.0))
                for b in range(B):
                    m = nc.vector.match_replace(pr[:, b, :], top8[:, b, :], pe_[:, b, :], 0.0)
                link(m)
                link(nc.vector.tensor_reduce(row_sum[:], top8[:, :, 0:top], AX_X, ALU.add))
                link(nc.vector.reciprocal(row_inv[:], row_sum[:]))
                link(nc.vector.tensor_tensor(ex, pe_[:, :, 0:experts], pr[:, :, 0:experts], ALU.subtract))
                nc.vector.tensor_tensor(comb[:, :, 0:experts], ex, over(row_inv[:], experts), ALU.mult
                                        ).then_inc(comb_ready, 1)
                dve.wait_ge(comb_turned, layer + 1)
                for g in range(2):
                    cols = slice(g * HALF, (g + 1) * HALF)
                    bank = ps_o[1 + g][0:experts, :]
                    link(nc.vector.tensor_copy(comb_hi[0:experts, cols], bank))
                    m = nc.vector.tensor_tensor(comb_lo[0:experts, cols], bank, comb_hi[0:experts, cols].bitcast(F32),
                                                ALU.subtract)
                m.then_inc(comb_split, 1)
                dve.wait_ge(comb_split, layer + 1)

            def copy_comb(n, rows):
                dve.wait_ge(comb_in, n)
                nc.vector.tensor_copy(comb_cur[0:rows, :], comb_next[0:rows, :]).then_inc(comb_copied, 1)

            def step(half, step_no, sel_no):
                dve.wait_ge(act_done, step_no + 1 + CREDIT)
                if sel_no is not None:
                    dve.wait_ge(sel_done, sel_no)
                dve.wait_ge(lo_done, step_no + 1)
                nc.vector.tensor_tensor(hid[:, half, :], ps_c[half][:], act_out[:, half, :], ALU.mult).then_inc(mult_done, 1)
                dve.wait_ge(hi_done, step_no + 1)
                nc.vector.tensor_tensor(hid_lo[:, half, :], hid[:, half, :], hid_hi[:, half, :].bitcast(F32),
                                        ALU.subtract).then_inc(lo_done, 1)

            def outputs(layer):
                for half in range(2):
                    dve.wait_ge(down_done, (STEPS0, LAST)[layer] + CREDIT)
                    nc.vector.tensor_scalar(y_t[:, 1, half * HALF:(half + 1) * HALF], ps_o[2 + half][:],
                                            tanh_g[:, 2 + layer:3 + layer], None, ALU.mult).then_inc(y_ready_dve, 1)
                for q in range(PAIRS):
                    dve.wait_ge(y_turned, PAIRS * layer + q + 1)
                    pair = xs[:, 2 * q:2 * q + 2, :].rearrange("p b d -> p (b d)")
                    m = nc.vector.tensor_tensor(pair, ps_t[q][:], pair, ALU.add)
                    m.then_inc(out_ready, 1)
                dve.wait_ge(out_ready, PAIRS * (layer + 1))

            nc.vector.memset(masked, NEG)
            nc.vector.memset(pext[0][:], -1.0)
            nc.vector.memset(pext[1][:], -1.0)
            link(nc.vector.memset(stats[:], 0.0))
            layernorm(0)
            link(nc.vector.memset(ones_f[:], 1.0))
            nc.vector.tensor_copy(ones2[:], ones_f[:])
            dve.wait_ge(sel_in, 16)
            link(nc.vector.tensor_copy(sel[:], sel_f[:]))
            dve.wait_ge(small_in, 16 * 8)
            link(nc.vector.tensor_reduce(valid_u8[:], mask_sb[:], AX_X, ALU.max))
            for g in range(2):
                dve.wait_ge(score0_ready, g + 1)
                part = masked[:, 4 * g:4 * g + 4, :]
                link(nc.vector.copy_predicated(part, mask_sb[:, 4 * g:4 * g + 4, :],
                                               ps_o[g][:].rearrange("p (b s) -> p b s", b=4)))
                link(nc.vector.tensor_reduce(row_max[:, 4 * g:4 * g + 4], part, AX_X, ALU.max))
                nc.vector.tensor_scalar(neg_max[:, 4 * g:4 * g + 4], row_max[:, 4 * g:4 * g + 4], -float(D) ** -0.5, None,
                                        ALU.mult).then_inc(max_ready, 1)
            dve.wait_ge(probs_ready, B)
            link(nc.vector.reciprocal(row_inv[:], row_sum[:]))
            dve.wait_ge(gains_ready, 1)
            link(nc.vector.scalar_tensor_tensor(row_gain[:], row_inv[:], tanh_g[:, 0:1], valid_u8[:], ALU.mult, ALU.mult))
            for b in range(B):
                dve.wait_ge(read0_ready, 2 * (b // 2) + 2)
                m = nc.vector.scalar_tensor_tensor(xs[:, b, :], ps_t[b // 2][:, (b % 2) * D:(b % 2 + 1) * D],
                                                   row_gain[:, b:b + 1], xs[:, b, :], ALU.mult, ALU.add)
            link(m)
            layernorm(1)
            lower_half(0)
            router(0)
            with dve.Fori(0, ROUNDS) as i:
                copy_comb(i * 32 + 32, 2 * EPR0)
                for s in range(2 * CH0):
                    step(s % 2, i * (2 * CH0) + s, i * 2 + (s + 1) if s < 2 else None)
            outputs(0)
            layernorm(2)
            for b in range(B):
                dve.wait_ge(read1_ready, 2 * (b // 2) + 2)
                m = nc.vector.scalar_tensor_tensor(xs[:, b, :], ps_o[b // 2][:, (b % 2) * D:(b % 2 + 1) * D],
                                                   tanh_g[:, 1:2], xs[:, b, :], ALU.mult, ALU.add)
            link(m)
            layernorm(3)
            lower_half(1)
            router(1)
            for s in range(STEPSH):
                step(s % 2, BASE_SH + s, 2 * ROUNDS + s + 1)
            with dve.Fori(0, ROUNDS) as i:
                copy_comb(i * 32 + (ROUNDS + 1) * 32, 2 * EPR1)
                for s in range(2 * CH1):
                    step(s % 2, i * (2 * CH1) + (BASE1 + s), i * (2 * CH1) + (2 * ROUNDS + STEPSH + s + 1))
            outputs(1)


def kernel(**inputs):
    import numpy as np
    import concourse.bacc as bacc
    from concourse.bass_utils import run_bass_kernel_spmd

    a = {k: np.ascontiguousarray(v) for k, v in inputs.items()}

    def up_layout(rows):
        return rows.reshape(-1, P, KD, P).transpose(0, 3, 2, 1).reshape(-1, P, D)

    def padded(rows):
        return np.concatenate([rows, np.zeros((SHC * P - rows.shape[0], rows.shape[1]), rows.dtype)])

    gu = a["L1_ffn_shared_gate_up"]
    down = padded(a["L1_ffn_shared_down"].T).reshape(SHC, P, D)
    sel_rows = np.zeros((2, EPR1, CH1 * P), np.float32)
    sel_rows[:, np.arange(CH1 * P) // I1, np.arange(CH1 * P)] = 1.0
    arrays = {
        "x": a["x"],
        "ctx": a["ctx_2048"],
        "ctx_t": a["ctx_2048"].reshape(B, S, KD, P).transpose(3, 0, 2, 1),
        "mask": a["mask_BxS2_bk0"],
        "g_xattn": a["g_xattn"],
        "g_ffn": a["g_ffn"],
        "gate0": a["L0_ffn_gate_w"].reshape(KD, P, E0).transpose(1, 0, 2),
        "gate0_b": a["L0_ffn_gate_b"],
        "w0": np.concatenate([up_layout(a["L0_ffn_w1"].transpose(0, 2, 1).reshape(E0 * F0, D)),
                              a["L0_ffn_w2"].reshape(-1, P, D)], axis=2),
        "b1": a["L0_ffn_b1"].reshape(-1, P).T,
        "b2": a["L0_ffn_b2"],
        "gate1": a["L1_ffn_gate_w"].reshape(E1, KD, P).transpose(2, 1, 0),
        "w1": np.concatenate([up_layout(a["L1_ffn_experts_w1"].reshape(E1 * I1, D)),
                              a["L1_ffn_experts_w2"].transpose(0, 2, 1).reshape(-1, P, D)], axis=2),
        "w_shared": np.concatenate([np.concatenate([up_layout(padded(gu[:SH1])), down], axis=2),
                                    np.concatenate([up_layout(padded(gu[SH1:])), np.zeros_like(down)], axis=2)]),
        "sel_rows": sel_rows.reshape(2 * EPR1, CH1, P),
    }
    nc = bacc.Bacc("TRN2", target_bir_lowering=False, num_devices=1)
    args = {}
    for name, v in arrays.items():
        arrays[name] = v = np.ascontiguousarray(v)
        args[name] = nc.dram_tensor(f"in_{name}", v.shape, mybir.dt.from_np(v.dtype), kind="ExternalInput").ap()
    out = nc.dram_tensor("out_x", (B, S, D), F32, kind="ExternalOutput").ap()
    flamingo_kernel(nc, **args, out=out)
    r = run_bass_kernel_spmd(nc, [{f"in_{k}": v for k, v in arrays.items()}], core_ids=[0])
    return r.results[0]["out_x"]
```

```python
import concourse.bass as bass
from concourse import mybir
from contextlib import ExitStack

F32 = mybir.dt.float32
F32R = mybir.dt.float32r
U8 = mybir.dt.uint8
ALU = mybir.AluOpType
ACT = mybir.ActivationFunctionType
AX_X = mybir.AxisListType.X

P = 128
B, S, D = 8, 128, 256
KD = D // P
TOK = B * S
HALF = TOK // 2
PAIRS = B // 2

E0, F0, TOP0 = 8, 1024, 2
E1, I1, TOP1, SH1 = 64, 176, 6, 352
EPS = 1e-5
NEG = -1e30

ROUNDS = 8
CH0 = F0 // P
EPR0 = E0 // ROUNDS
EPR1 = E1 // ROUNDS
CH1 = EPR1 * I1 // P
SHC = -(-SH1 // P)
SLOTS = CH1
CSLOTS = 4
SPAN0 = CH0 // 2
COMB_AT = 3
STEPS0, STEPSH, STEPS1 = 2 * CH0 * ROUNDS, 2 * SHC, 2 * CH1 * ROUNDS
BASE_SH = STEPS0
BASE1 = STEPS0 + STEPSH
LAST = STEPS0 + STEPSH + STEPS1
WB_SH = CH0 * ROUNDS
WB1 = WB_SH + 2 * SHC
CREDIT = 2


def loads_before(layer, slot):
    if layer == 0:
        return 0
    return (ROUNDS if slot < CH0 else 0) + (1 if slot < 2 * SHC else 0)


def pieces(t):
    found, row = [], t * P
    while row < (t + 1) * P:
        expert = row // I1
        end = min((expert + 1) * I1, (t + 1) * P)
        found.append((expert, row - t * P, end - t * P))
        row = end
    return found


def spread_loads(slot, chunks):
    return sum(len(pieces(t)) for t in range(chunks) if t % CSLOTS == slot)


def flamingo_kernel(nc, x, ctx, ctx_t, mask, g_xattn, g_ffn, gate0, gate0_b, w0, b1, b2,
                    gate1, w1, w_shared, out):
    comb_rows = nc.dram_tensor("comb_rows", (2, E1, TOK), F32).ap()

    with ExitStack() as stack:
        def sb(name, shape, dt=F32):
            return stack.enter_context(nc.sbuf_tensor(name, shape, dt))

        def sem(name):
            return stack.enter_context(nc.semaphore(name))

        xs = sb("xs", [P, B, D])
        xn = sb("xn", [P, B, D])
        xn_t = sb("xn_t", [P, KD, TOK])
        xt_hi = sb("xt_hi", [P, KD, TOK], F32R)
        xt_lo = sb("xt_lo", [P, KD, TOK], F32R)
        ctx_sb = sb("ctx_sb", [P, B, D])
        ctx_tsb = sb("ctx_tsb", [P, B, KD, S])
        mask_sb = sb("mask_sb", [P, B, S], U8)
        ident = sb("ident", [P, P])
        gains = sb("gains", [P, 4])
        tanh_g = sb("tanh_g", [P, 4])
        valid_u8 = sb("valid_u8", [P, B])
        row_max = sb("row_max", [P, B])
        neg_max = sb("neg_max", [P, B])
        row_sum = sb("row_sum", [P, B])
        row_inv = sb("row_inv", [P, B])
        row_gain = sb("row_gain", [P, B])
        stats = sb("stats", [P, B, 6])
        mean_var = sb("mean_var", [P, B, 2])
        std = sb("std", [P, B])
        rstd = sb("rstd", [P, B])
        gate_sb = [sb("gate0_sb", [P, KD, E0]), sb("gate1_sb", [P, KD, E1])]
        gate_b_sb = sb("gate_b_sb", [P, E0])
        b1_sb = sb("b1_sb", [P, WB_SH])
        b1_round = sb("b1_round", [P, CH0])
        b2_sb = sb("b2_sb", [E0, D])
        stage = sb("stage", [P, SLOTS, 2 * D])
        w_hi = sb("w_hi", [P, SLOTS, 2 * D], F32R)
        w_lo = sb("w_lo", [P, SLOTS, 2 * D], F32R)
        hid_hi = sb("hid_hi", [P, 2, HALF], F32R)
        hid_lo = sb("hid_lo", [P, 2, HALF], F32R)
        y_t = sb("y_t", [P, KD, TOK])
        masked = y_t[:, 0, :].rearrange("p (b s) -> p b s", b=B)
        probs = y_t[:, 1, :].rearrange("p (b s) -> p b s", b=B)
        shared_act = y_t[:, 0, :].rearrange("p (h t) -> p h t", h=2)
        shared_hid = y_t[:, 1, :].rearrange("p (h t) -> p h t", h=2)
        probs_t = sb("probs_t", [P, B, S])
        score1 = sb("score1", [P, 2, 2 * D])
        logit = sb("logit", [P, B * E1])
        expo = sb("expo", [P, B * E1])
        pext = [sb("pext0", [P, B, E0 + 8 - TOP0]), sb("pext1", [P, B, E1 + 8 - TOP1])]
        prep = [sb("prep0", [P, B, E0 + 8 - TOP0]), sb("prep1", [P, B, E1 + 8 - TOP1])]
        top8 = sb("top8", [P, B, 8])
        comb = sb("comb", [P, B, E1])
        comb_t = sb("comb_t", [E1, TOK])
        comb_b = sb("comb_b", [P, CSLOTS, TOK])
        zero = sb("zero", [P, 1])
        scratch = sb("scratch", [P, 4])

        ps_h = [stack.enter_context(nc.psum_tensor(f"ps_h{i}", [P, HALF], F32)) for i in range(2)]
        ps_a = [stack.enter_context(nc.psum_tensor(f"ps_a{i}", [P, HALF], F32)) for i in range(2)]
        ps_o = [stack.enter_context(nc.psum_tensor(f"ps_o{i}", [P, HALF], F32)) for i in range(4)]
        ps_t = ps_h + ps_a

        x_in = [sem(f"x_in{q}") for q in range(PAIRS)]
        ctx_in, ctx_t_in, small_in = (sem(n) for n in ("ctx_in", "ctx_t_in", "small_in"))
        const_ready = sem("const_ready")
        vec = sem("vec")
        gains_ready, var_ready, std_ready, xn_ready = (sem(n) for n in ("gains_ready", "var_ready", "std_ready", "xn_ready"))
        xn_turned, xn_t_ready, xt_hi_ready, xt_lo_ready = (sem(n) for n in ("xn_turned", "xn_t_ready", "xt_hi_ready", "xt_lo_ready"))
        score0_ready, max_ready, probs_ready, probs_turned, probs_t_ready, read0_ready = (
            sem(n) for n in ("score0_ready", "max_ready", "probs_ready", "probs_turned", "probs_t_ready", "read0_ready"))
        score1_done, score1_ready, read1_ready, read1_used = (sem(n) for n in ("score1_done", "score1_ready", "read1_ready", "read1_used"))
        logits_done, shifted_ready, expo_ready, comb_ready, comb_turned, comb_t_ready, comb_out = (
            sem(n) for n in ("logits_done", "shifted_ready", "expo_ready", "comb_ready", "comb_turned", "comb_t_ready", "comb_out"))
        w_in = [sem(f"w_in{t}") for t in range(SLOTS)]
        w_split = sem("w_split")
        comb_in = [sem(f"comb_in{c}") for c in range(CSLOTS)]
        up_done, linear_done, act_done, mult_done, hi_done, lo_done, down_done = (
            sem(n) for n in ("up_done", "linear_done", "act_done", "mult_done", "hi_done", "lo_done", "down_done"))
        y_ready_act, y_ready_dve, y_turned, out_ready, stored = (
            sem(n) for n in ("y_ready_act", "y_ready_dve", "y_turned", "out_ready", "stored"))
        split_hi, bias_ready = sem("split_hi"), sem("bias_ready")

        block = stack.enter_context(nc.Block())

        @block.sync
        def _(sp):
            for q in range(PAIRS):
                sp.dma_start(xs[:, 2 * q:2 * q + 2, :], x[2 * q:2 * q + 2].rearrange("b s d -> s b d")).then_inc(x_in[q], 16)
            sp.dma_start(ctx_tsb[:], ctx_t).then_inc(ctx_t_in, 16)
            sp.dma_start(ctx_sb[:], ctx.rearrange("b s d -> s b d")).then_inc(ctx_in, 16)
            for dst, src in ((gate_sb[0][:], gate0), (gate_sb[1][:], gate1), (gate_b_sb[:], gate0_b.partition_broadcast(P)),
                             (b1_sb[:], b1), (b2_sb[:], b2)):
                sp.dma_start(dst, src).then_inc(small_in, 16)

            def load_weights(block, t, split_no):
                if split_no is not None:
                    sp.wait_ge(w_split, split_no)
                sp.dma_start(stage[:, t, :], block).then_inc(w_in[t], 16)

            def spread0(i, part, steps_done):
                if steps_done is not None:
                    sp.wait_ge(mult_done, steps_done)
                sp.dma_start(comb_b[:, part, :], comb_rows[0, i].partition_broadcast(P)).then_inc(comb_in[part], 16)

            def spread1(i, t, steps_done):
                if steps_done is not None:
                    sp.wait_ge(mult_done, steps_done)
                for expert, first, end in pieces(t):
                    sp.dma_start(comb_b[first:end, t % CSLOTS, :],
                                 comb_rows1[i, expert].partition_broadcast(end - first)).then_inc(comb_in[t % CSLOTS], 16)

            def round0(i, first, last):
                for t in range(CH0):
                    if t % SPAN0 == 0:
                        spread0(i, t // SPAN0, None if first else
                                (i - 1) * (2 * CH0) + (2 * (t + SPAN0) + CREDIT))
                    if not last:
                        load_weights(w0_v[i + 1, t], t, i * CH0 + (t + 1))
                    elif t < 2 * SHC:
                        load_weights(w_shared[t], t, i * CH0 + (t + 1))
                    else:
                        load_weights(w1_v[0, t], t, i * CH0 + (t + 1))

            def round1(i, first, last):
                for t in range(CH1):
                    if t >= CSLOTS:
                        free = i * (2 * CH1) + (BASE1 + 2 * (t - CSLOTS + 1) + CREDIT)
                    elif first:
                        free = STEPS0 + CREDIT
                    else:
                        before = max(u for u in range(CH1) if u % CSLOTS == t)
                        free = (i - 1) * (2 * CH1) + (BASE1 + 2 * (before + 1) + CREDIT)
                    spread1(i, t, free)
                    if not last:
                        load_weights(w1_v[i + 1, t], t, i * CH1 + (WB1 + t + 1))

            w0_v = w0.rearrange("(i t) p n -> i t p n", t=CH0)
            w1_v = w1.rearrange("(i t) p n -> i t p n", t=CH1)
            comb_rows1 = comb_rows[1].rearrange("(i e) t -> i e t", e=EPR1)
            for t in range(CH0):
                load_weights(w0_v[0, t], t, None)
            for t in range(CH0, CH1):
                load_weights(w1_v[0, t], t, None)
            sp.wait_ge(comb_out, 16)
            round0(0, True, False)
            with sp.Fori(1, ROUNDS - 1) as i:
                round0(i, False, False)
            round0(ROUNDS - 1, False, True)
            for t in range(2 * SHC):
                load_weights(w1_v[0, t], t, WB_SH + t + 1)
            sp.wait_ge(comb_out, 32)
            round1(0, True, False)
            with sp.Fori(1, ROUNDS - 1) as i:
                round1(i, False, False)
            round1(ROUNDS - 1, False, True)
            for q in range(PAIRS):
                sp.wait_ge(out_ready, PAIRS + q + 1)
                sp.dma_start(out[2 * q:2 * q + 2].rearrange("b s d -> s b d"), xs[:, 2 * q:2 * q + 2, :]).then_inc(stored, 16)
            sp.wait_ge(stored, 16 * PAIRS)

        @block.gpsimd
        def _(pool):
            pool.memset(zero[:], 0.0).then_inc(const_ready, 1)
            pool.memset(ident[:], 0.0).then_inc(const_ready, 1)
            pool.wait_ge(const_ready, 2)
            pool.affine_select(out=ident[:], in_=ident[:], compare_op=ALU.not_equal, fill=1.0, base=0,
                               pattern=[[-1, P]], channel_multiplier=1).then_inc(const_ready, 1)
            pool.memset(scratch[:, 0:1], 0.0).then_inc(act_done, CREDIT)
            pool.memset(scratch[:, 1:2], 0.0).then_inc(mult_done, CREDIT)
            pool.memset(scratch[:, 2:3], 0.0).then_inc(down_done, CREDIT)
            pool.memset(scratch[:, 3:4], 0.0).then_inc(lo_done, CREDIT)

            def split(t, loads, block_no, free_after):
                pool.wait_ge(w_in[t], 16 * loads)
                if free_after is not None:
                    pool.wait_ge(down_done, free_after)
                pool.tensor_tensor(w_hi[:, t, :], stage[:, t, :], zero[:].broadcast_to([P, 2 * D]), ALU.add).then_inc(split_hi, 1)
                pool.wait_ge(split_hi, block_no + 1)
                pool.tensor_tensor(w_lo[:, t, :], stage[:, t, :], w_hi[:, t, :].bitcast(F32), ALU.subtract
                                   ).then_inc(w_split, 1)

            def after_step(step):
                return step + 1 + CREDIT

            def lower_half(n):
                for q in range(PAIRS):
                    pool.wait_ge(xt_hi_ready, PAIRS * n + q + 1)
                    cols = slice(q * 2 * S, (q + 1) * 2 * S)
                    pool.tensor_tensor(xt_lo[:, :, cols], xn_t[:, :, cols], xt_hi[:, :, cols].bitcast(F32),
                                       ALU.subtract).then_inc(xt_lo_ready, 1)

            for t in range(CH0):
                split(t, 1, t, None)
            lower_half(0)
            with pool.Fori(1, ROUNDS) as i:
                for t in range(CH0):
                    split(t, i + 1, i * CH0 + t, (i - 1) * (2 * CH0) + after_step(2 * t + 1))
            for j in range(2 * SHC):
                split(j, ROUNDS + 1, WB_SH + j, after_step(2 * ((ROUNDS - 1) * CH0 + j) + 1))
            lower_half(1)
            for t in range(CH1):
                if t < 2 * SHC:
                    free = after_step(BASE_SH + 2 * (t % SHC) + 1)
                elif t < CH0:
                    free = after_step(2 * ((ROUNDS - 1) * CH0 + t) + 1)
                else:
                    free = None
                split(t, loads_before(1, t) + 1, WB1 + t, free)
            with pool.Fori(1, ROUNDS) as i:
                for t in range(CH1):
                    split(t, i + (loads_before(1, t) + 1), i * CH1 + (WB1 + t),
                          (i - 1) * (2 * CH1) + after_step(BASE1 + 2 * t + 1))

        @block.tensor
        def _(pe):
            def turn_norm(n):
                for q in range(PAIRS):
                    for b in (2 * q, 2 * q + 1):
                        pe.wait_ge(xn_ready, (0, 1, 3)[n] * B + b + 1)
                        for k in range(KD):
                            m = nc.tensor.transpose(ps_t[q][:, k * 2 * S + (b % 2) * S:k * 2 * S + (b % 2 + 1) * S],
                                                    xn[:, b, k * P:(k + 1) * P], ident[:])
                    m.then_inc(xn_turned, 1)

            def three(dst, w, w_cols, moving, m_cols, start, stop):
                (hi_w, lo_w), (hi_m, lo_m) = w, moving
                nc.tensor.matmul(dst, w_cols(hi_w), m_cols(hi_m), start=start, stop=False)
                nc.tensor.matmul(dst, w_cols(hi_w), m_cols(lo_m), start=False, stop=False)
                return nc.tensor.matmul(dst, w_cols(lo_w), m_cols(hi_m), start=False, stop=stop)

            def up(dst, t, half, first_col):
                for k in range(KD):
                    m = three(dst, (w_hi, w_lo), lambda w: w[:, t, first_col + k * P:first_col + (k + 1) * P],
                              (xt_hi, xt_lo), lambda v: v[:, k, half * HALF:(half + 1) * HALF], k == 0, k == KD - 1)
                return m

            def down(t, half, start, stop):
                for d in range(KD):
                    m = three(ps_o[2 * d + half][:], (w_hi, w_lo), lambda w: w[:, t, D + d * P:D + (d + 1) * P],
                              (hid_hi, hid_lo), lambda v: v[:, half, :], start, stop)
                m.then_inc(down_done, 1)

            def up_step(half, t, step, block_no):
                if half == 0:
                    pe.wait_ge(w_split, block_no + 1)
                pe.wait_ge(act_done, step + 1)
                up(ps_h[half][:], t, half, 0).then_inc(up_done, 1)

            def round_steps(layer, i, last):
                chunks = CH0 if layer == 0 else CH1
                base = 0 if layer == 0 else BASE1
                wbase = 0 if layer == 0 else WB1
                steps = 2 * chunks
                for s in range(steps):
                    ahead = s + 2
                    wrap = ahead >= steps
                    t, half = (ahead % steps) // 2, s % 2
                    if not (last and wrap):
                        up_step(half, t, i * steps + (base + ahead), i * chunks + (wbase + ahead // 2))
                    pe.wait_ge(lo_done, i * steps + (base + s + 1 + CREDIT))
                    down(s // 2, half, False, last and s >= steps - 2)

            def rounds(layer):
                with pe.Fori(0, ROUNDS - 1) as i:
                    round_steps(layer, i, False)
                round_steps(layer, ROUNDS - 1, True)

            def logits(layer, bank):
                experts = (E0, E1)[layer]
                for b in range(B):
                    pe.wait_ge(xn_t_ready, PAIRS * (layer + 1) + b // 2 + 1)
                    for k in range(KD):
                        m = nc.tensor.matmul(bank[:, b * experts:(b + 1) * experts],
                                             xn_t[:, k, b * S:(b + 1) * S], gate_sb[layer][:, k, :],
                                             start=(k == 0), stop=(k == KD - 1))
                m.then_inc(logits_done, 1)

            def turn_comb(layer, banks):
                experts = (E0, E1)[layer]
                pe.wait_ge(comb_ready, layer + 1)
                for b in range(B):
                    m = nc.tensor.transpose(banks[b // 4][0:experts, (b % 4) * S:(b % 4 + 1) * S],
                                            comb[:, b, 0:experts], ident[:])
                m.then_inc(comb_turned, 1)

            def read1(b):
                pe.wait_ge(score1_ready, b + 1)
                for k in range(KD):
                    m = nc.tensor.matmul(ps_o[b // 2][:, (b % 2) * D:(b % 2 + 1) * D], ctx_tsb[:, b, k, :],
                                         score1[:, b % 2, k * D:(k + 1) * D], start=(k == 0), stop=(k == KD - 1))
                m.then_inc(read1_ready, 1)

            def turn_output(layer):
                pe.wait_ge(y_ready_act, 2 * (layer + 1))
                pe.wait_ge(y_ready_dve, 2 * (layer + 1))
                for b in range(B):
                    for d in range(KD):
                        m = nc.tensor.transpose(ps_t[b // 2][:, (b % 2) * D + d * P:(b % 2) * D + (d + 1) * P],
                                                y_t[:, d, b * S:(b + 1) * S], ident[:])
                    if b % 2:
                        m.then_inc(y_turned, 1)

            pe.wait_ge(const_ready, 3)
            turn_norm(0)
            pe.wait_ge(ctx_t_in, 16)
            for b in range(B):
                pe.wait_ge(xn_t_ready, b // 2 + 1)
                for k in range(KD):
                    m = nc.tensor.matmul(ps_o[b // 4][:, (b % 4) * S:(b % 4 + 1) * S], xn_t[:, k, b * S:(b + 1) * S],
                                         ctx_tsb[:, b, k, :], start=(k == 0), stop=(k == KD - 1))
                if b % 4 == 3:
                    m.then_inc(score0_ready, 1)
            for b in range(B):
                pe.wait_ge(probs_ready, b + 1)
                m = nc.tensor.transpose(ps_o[2 + b // 4][:, (b % 4) * S:(b % 4 + 1) * S], probs[:, b, :], ident[:])
                if b % 4 == 3:
                    m.then_inc(probs_turned, 1)
            pe.wait_ge(ctx_in, 16)
            for b in range(B):
                pe.wait_ge(probs_t_ready, b // 4 + 1)
                nc.tensor.matmul(ps_t[b // 2][:, (b % 2) * D:(b % 2 + 1) * D], probs_t[:, b, :], ctx_sb[:, b, :],
                                 start=True, stop=True).then_inc(read0_ready, 1)
            turn_norm(1)
            logits(0, ps_o[0])
            for half in range(2):
                pe.wait_ge(xt_lo_ready, 2 * half + 2)
                up_step(half, 0, half, 0)
            turn_comb(0, ps_o[1:3])
            pe.wait_ge(comb_t_ready, 2)
            for d in range(KD):
                for half in range(2):
                    nc.tensor.matmul(ps_o[2 * d + half][:], b2_sb[:, d * P:(d + 1) * P],
                                     comb_t[0:E0, half * HALF:(half + 1) * HALF], start=True, stop=False)
            rounds(0)
            turn_output(0)
            for b in range(B):
                pe.wait_ge(xn_ready, 2 * B + b + 1)
                if b >= 4:
                    pe.wait_ge(score1_ready, b - 3)
                for k in range(KD):
                    m = nc.tensor.matmul(ps_t[b % 4][:, k * D:(k + 1) * D], xn[:, b, k * P:(k + 1) * P],
                                         ctx_sb[:, b, :], start=True, stop=True)
                m.then_inc(score1_done, 1)
                if b >= 1:
                    read1(b - 1)
            read1(B - 1)
            turn_norm(2)
            pe.wait_ge(xn_t_ready, 3 * PAIRS)
            logits(1, ps_a[0])
            for s in range(STEPSH):
                if s < 2:
                    pe.wait_ge(xt_lo_ready, PAIRS + 2 * s + 2)
                if s % 2 == 0:
                    pe.wait_ge(w_split, WB_SH + s // 2 + 1)
                pe.wait_ge(act_done, BASE_SH + s + CREDIT)
                up(ps_h[0][:], s // 2, s % 2, 0).then_inc(up_done, 1)
                if s % 2 == 0:
                    pe.wait_ge(w_split, WB_SH + SHC + s // 2 + 1)
                pe.wait_ge(mult_done, BASE_SH + s + CREDIT)
                up(ps_h[1][:], SHC + s // 2, s % 2, 0).then_inc(linear_done, 1)
                if s >= 1:
                    pe.wait_ge(lo_done, BASE_SH + s + CREDIT)
                    down((s - 1) // 2, (s - 1) % 2, s < 3, False)
                if s == COMB_AT:
                    turn_comb(1, ps_a)
            pe.wait_ge(act_done, BASE1 + CREDIT)
            up_step(0, 0, BASE1, WB1)
            pe.wait_ge(mult_done, BASE1 + CREDIT)
            up_step(1, 0, BASE1 + 1, WB1)
            pe.wait_ge(lo_done, BASE1 + CREDIT)
            down(SHC - 1, 1, False, False)
            rounds(1)
            turn_output(1)

        @block.scalar
        def _(act):
            def root(n):
                for g in range(2):
                    act.wait_ge(var_ready, 2 * n + g + 1)
                    nc.scalar.activation(std[:, 4 * g:4 * g + 4], mean_var[:, 4 * g:4 * g + 4, 1], ACT.Sqrt
                                         ).then_inc(std_ready, 1)

            def take_turned(n):
                for q in range(PAIRS):
                    act.wait_ge(xn_turned, PAIRS * n + q + 1)
                    nc.scalar.activation(xn_t[:, :, q * 2 * S:(q + 1) * 2 * S],
                                         ps_t[q][:].rearrange("p (k t) -> p k t", k=KD), ACT.Copy).then_inc(xn_t_ready, 1)
                for q in range(PAIRS if n > 0 else 0):
                    act.wait_ge(xn_t_ready, PAIRS * n + q + 1)
                    nc.scalar.activation(xt_hi[:, :, q * 2 * S:(q + 1) * 2 * S],
                                         xn_t[:, :, q * 2 * S:(q + 1) * 2 * S], ACT.Copy).then_inc(xt_hi_ready, 1)

            def exponent(layer):
                act.wait_ge(shifted_ready, layer + 1)
                n = B * (E0, E1)[layer]
                nc.scalar.activation(expo[:, 0:n], logit[:, 0:n], ACT.Exp).then_inc(expo_ready, 1)

            def take_comb(layer, banks):
                experts = (E0, E1)[layer]
                act.wait_ge(comb_turned, layer + 1)
                for g in range(2):
                    nc.scalar.activation(comb_t[0:experts, g * HALF:(g + 1) * HALF], banks[g][0:experts, :], ACT.Copy
                                         ).then_inc(comb_t_ready, 1)
                act.wait_ge(comb_t_ready, 2 * (layer + 1))
                act.dma_start(comb_rows[layer, 0:experts, :], comb_t[0:experts, :]).then_inc(comb_out, 16)

            def upper_half(half, step_no, hidden):
                act.wait_ge(mult_done, step_no + 1 + CREDIT)
                act.wait_ge(down_done, step_no + 1)
                nc.scalar.activation(hid_hi[:, half, :], hidden, ACT.Copy).then_inc(hi_done, 1)

            def step(half, step_no, func, bias):
                act.wait_ge(up_done, step_no + 1)
                act.wait_ge(lo_done, step_no + 1)
                nc.scalar.activation(ps_a[half][:], ps_h[half][:], func, bias=bias).then_inc(act_done, 1)
                upper_half(half, step_no, ps_a[half][:])

            def shared_step(half, step_no):
                act.wait_ge(up_done, step_no + 1)
                act.wait_ge(lo_done, step_no + 1)
                nc.scalar.activation(shared_act[:, half, :], ps_h[0][:], ACT.Silu).then_inc(act_done, 1)
                upper_half(half, step_no, shared_hid[:, half, :])

            def outputs(layer):
                for half in range(2):
                    act.wait_ge(down_done, (STEPS0, LAST)[layer] + CREDIT)
                    nc.scalar.activation(y_t[:, 0, half * HALF:(half + 1) * HALF], ps_o[half][:], ACT.Copy,
                                         scale=tanh_g[:, 2 + layer:3 + layer]).then_inc(y_ready_act, 1)

            act.dma_start(mask_sb[:], mask.partition_broadcast(P)).then_inc(small_in, 16)
            act.dma_start(gains[:, 0:2], g_xattn.partition_broadcast(P)).then_inc(small_in, 16)
            act.dma_start(gains[:, 2:4], g_ffn.partition_broadcast(P)).then_inc(small_in, 16)
            root(0)
            act.wait_ge(small_in, 16 * 8)
            nc.scalar.activation(tanh_g[:], gains[:], ACT.Tanh).then_inc(gains_ready, 1)
            take_turned(0)
            for b in range(B):
                act.wait_ge(max_ready, b // 4 + 1)
                nc.scalar.activation(probs[:, b, :], masked[:, b, :], ACT.Exp, bias=neg_max[:, b:b + 1],
                                     scale=float(D) ** -0.5, accum_out=row_sum[:, b:b + 1]).then_inc(probs_ready, 1)
            for g in range(2):
                act.wait_ge(probs_turned, g + 1)
                nc.scalar.activation(probs_t[:, 4 * g:4 * g + 4, :].rearrange("p b s -> p (b s)"), ps_o[2 + g][:],
                                     ACT.Copy).then_inc(probs_t_ready, 1)
            root(1)
            take_turned(1)
            exponent(0)
            take_comb(0, ps_o[1:3])
            nc.scalar.preload_act_table(ACT.Gelu_apprx_tanh)
            with act.Fori(0, ROUNDS) as i:
                nc.scalar.activation(b1_round[:], b1_sb[:, bass.ds(i * CH0, CH0)], ACT.Copy).then_inc(bias_ready, 1)
                act.wait_ge(bias_ready, i + 1)
                for s in range(2 * CH0):
                    step(s % 2, i * (2 * CH0) + s, ACT.Gelu_apprx_tanh, b1_round[:, s // 2:s // 2 + 1])
            outputs(0)
            root(2)
            for b in range(B):
                act.wait_ge(score1_done, b + 1)
                if b >= 2:
                    act.wait_ge(read1_ready, b - 1)
                nc.scalar.activation(score1[:, b % 2, :], ps_t[b % 4][:], ACT.Sigmoid, scale=float(S) ** -0.5
                                     ).then_inc(score1_ready, 1)
            root(3)
            take_turned(2)
            exponent(1)
            for s in range(STEPSH):
                shared_step(s % 2, BASE_SH + s)
                if s == COMB_AT:
                    take_comb(1, ps_a)
            with act.Fori(0, ROUNDS) as i:
                for s in range(2 * CH1):
                    step(s % 2, i * (2 * CH1) + (BASE1 + s), ACT.Silu, 0.0)
            outputs(1)

        @block.vector
        def _(dve):
            count = [0]

            def link(ins):
                count[0] += 1
                ins.then_inc(vec, 1)
                dve.wait_ge(vec, count[0])

            def layernorm(n):
                for g in range(2):
                    part = slice(4 * g, 4 * g + 4)
                    for b in range(4 * g, 4 * g + 4):
                        if n == 0 and b % 2 == 0:
                            dve.wait_ge(x_in[b // 2], 16)
                        m = nc.vector.bn_stats(stats[:, b, :], xs[:, b, :])
                    link(m)
                    for b in range(4 * g, 4 * g + 4):
                        m = nc.vector.bn_aggr(mean_var[:, b, :], stats[:, b, :])
                    link(m)
                    nc.vector.tensor_scalar(mean_var[:, part, 1], mean_var[:, part, 1], EPS, None, ALU.add
                                            ).then_inc(var_ready, 1)
                for g in range(2):
                    part = slice(4 * g, 4 * g + 4)
                    dve.wait_ge(std_ready, 2 * n + g + 1)
                    link(nc.vector.reciprocal(rstd[:, part], std[:, part]))
                    for b in range(4 * g, 4 * g + 4):
                        nc.vector.tensor_scalar(xn[:, b, :], xs[:, b, :], mean_var[:, b, 0:1], rstd[:, b:b + 1],
                                                ALU.subtract, ALU.mult).then_inc(xn_ready, 1)
                dve.wait_ge(xn_ready, B * (n + 1))

            def over(v, n):
                return v.unsqueeze(2).broadcast_to([P, B, n])

            def routed(v, layer):
                return v[:, 0:B * (E0, E1)[layer]].rearrange("p (b e) -> p b e", b=B)

            def shift(layer, bank):
                experts = (E0, E1)[layer]
                lg, raw = routed(logit, layer), routed(bank, layer)
                dve.wait_ge(logits_done, layer + 1)
                if layer == 0:
                    link(nc.vector.tensor_tensor(lg, raw, gate_b_sb[:].unsqueeze(1).broadcast_to([P, B, E0]), ALU.add))
                else:
                    link(nc.vector.tensor_copy(lg, raw))
                link(nc.vector.tensor_reduce(row_max[:], lg, AX_X, ALU.max))
                nc.vector.tensor_tensor(lg, lg, over(row_max[:], experts), ALU.subtract).then_inc(shifted_ready, 1)

            def find_top(layer):
                experts, top = ((E0, TOP0), (E1, TOP1))[layer]
                ex, with_marks, without_top = routed(expo, layer), pext[layer], prep[layer]
                dve.wait_ge(expo_ready, layer + 1)
                link(nc.vector.tensor_reduce(row_sum[:], ex, AX_X, ALU.add))
                link(nc.vector.reciprocal(row_inv[:], row_sum[:]))
                link(nc.vector.tensor_tensor(with_marks[:, :, 0:experts], ex, over(row_inv[:], experts), ALU.mult))
                for b in range(B):
                    m = nc.vector.max(top8[:, b, :], with_marks[:, b, 0:experts])
                link(m)
                link(nc.vector.memset(top8[:, :, top:8], -1.0))
                for b in range(B):
                    m = nc.vector.match_replace(without_top[:, b, :], top8[:, b, :], with_marks[:, b, :], 0.0)
                link(m)

            def combine(layer):
                experts, top = ((E0, TOP0), (E1, TOP1))[layer]
                ex = routed(expo, layer)
                link(nc.vector.tensor_reduce(row_sum[:], top8[:, :, 0:top], AX_X, ALU.add))
                link(nc.vector.reciprocal(row_inv[:], row_sum[:]))
                link(nc.vector.tensor_tensor(ex, pext[layer][:, :, 0:experts], prep[layer][:, :, 0:experts], ALU.subtract))
                nc.vector.tensor_tensor(comb[:, :, 0:experts], ex, over(row_inv[:], experts), ALU.mult
                                        ).then_inc(comb_ready, 1)

            def lower(half, step_no, hidden):
                dve.wait_ge(hi_done, step_no + 1)
                nc.vector.tensor_tensor(hid_lo[:, half, :], hidden, hid_hi[:, half, :].bitcast(F32),
                                        ALU.subtract).then_inc(lo_done, 1)

            def step(half, step_no, slot, loads):
                dve.wait_ge(act_done, step_no + 1 + CREDIT)
                if loads is not None:
                    dve.wait_ge(comb_in[slot], loads)
                nc.vector.tensor_tensor(ps_a[half][:], ps_a[half][:], comb_b[:, slot, half * HALF:(half + 1) * HALF],
                                        ALU.mult).then_inc(mult_done, 1)
                lower(half, step_no, ps_a[half][:])

            def shared_step(half, step_no, linear_no):
                dve.wait_ge(act_done, step_no + 1 + CREDIT)
                dve.wait_ge(linear_done, linear_no + 1)
                nc.vector.tensor_tensor(shared_hid[:, half, :], ps_h[1][:], shared_act[:, half, :], ALU.mult
                                        ).then_inc(mult_done, 1)
                lower(half, step_no, shared_hid[:, half, :])

            def outputs(layer):
                for half in range(2):
                    dve.wait_ge(down_done, (STEPS0, LAST)[layer] + CREDIT)
                    nc.vector.tensor_scalar(y_t[:, 1, half * HALF:(half + 1) * HALF], ps_o[2 + half][:],
                                            tanh_g[:, 2 + layer:3 + layer], None, ALU.mult).then_inc(y_ready_dve, 1)
                for q in range(PAIRS):
                    dve.wait_ge(y_turned, PAIRS * layer + q + 1)
                    pair = xs[:, 2 * q:2 * q + 2, :].rearrange("p b d -> p (b d)")
                    m = nc.vector.tensor_tensor(pair, ps_t[q][:], pair, ALU.add)
                    m.then_inc(out_ready, 1)
                dve.wait_ge(out_ready, PAIRS * (layer + 1))

            nc.vector.memset(masked, NEG)
            nc.vector.memset(pext[0][:], -1.0)
            nc.vector.memset(pext[1][:], -1.0)
            link(nc.vector.memset(stats[:], 0.0))
            layernorm(0)
            dve.wait_ge(small_in, 16 * 8)
            link(nc.vector.tensor_reduce(valid_u8[:], mask_sb[:], AX_X, ALU.max))
            for g in range(2):
                dve.wait_ge(score0_ready, g + 1)
                part = masked[:, 4 * g:4 * g + 4, :]
                link(nc.vector.copy_predicated(part, mask_sb[:, 4 * g:4 * g + 4, :],
                                               ps_o[g][:].rearrange("p (b s) -> p b s", b=4)))
                link(nc.vector.tensor_reduce(row_max[:, 4 * g:4 * g + 4], part, AX_X, ALU.max))
                nc.vector.tensor_scalar(neg_max[:, 4 * g:4 * g + 4], row_max[:, 4 * g:4 * g + 4], -float(D) ** -0.5, None,
                                        ALU.mult).then_inc(max_ready, 1)
            dve.wait_ge(probs_ready, B)
            link(nc.vector.reciprocal(row_inv[:], row_sum[:]))
            dve.wait_ge(gains_ready, 1)
            link(nc.vector.scalar_tensor_tensor(row_gain[:], row_inv[:], tanh_g[:, 0:1], valid_u8[:], ALU.mult, ALU.mult))
            for b in range(B):
                dve.wait_ge(read0_ready, 2 * (b // 2) + 2)
                m = nc.vector.scalar_tensor_tensor(xs[:, b, :], ps_t[b // 2][:, (b % 2) * D:(b % 2 + 1) * D],
                                                   row_gain[:, b:b + 1], xs[:, b, :], ALU.mult, ALU.add)
            link(m)
            layernorm(1)
            shift(0, ps_o[0])
            find_top(0)
            combine(0)
            with dve.Fori(0, ROUNDS) as i:
                for s in range(2 * CH0):
                    chunk = s // 2
                    step(s % 2, i * (2 * CH0) + s, chunk // SPAN0, i * 16 + 16 if s % (2 * SPAN0) == 0 else None)
            outputs(0)
            layernorm(2)
            for b in range(B):
                dve.wait_ge(read1_ready, 2 * (b // 2) + 2)
                m = nc.vector.scalar_tensor_tensor(xs[:, b, :], ps_o[b // 2][:, (b % 2) * D:(b % 2 + 1) * D],
                                                   tanh_g[:, 1:2], xs[:, b, :], ALU.mult, ALU.add)
            link(m)
            layernorm(3)
            shift(1, ps_a[0])
            find_top(1)
            shared_step(0, BASE_SH, 0)
            combine(1)
            for s in range(1, STEPSH):
                shared_step(s % 2, BASE_SH + s, s)
            with dve.Fori(0, ROUNDS) as i:
                for s in range(2 * CH1):
                    chunk, slot = s // 2, s // 2 % CSLOTS
                    layer0 = ROUNDS if slot < CH0 // SPAN0 else 0
                    loads = (i * (16 * spread_loads(slot, CH1)) + 16 * (layer0 + spread_loads(slot, chunk + 1))
                             if s % 2 == 0 else None)
                    step(s % 2, i * (2 * CH1) + (BASE1 + s), slot, loads)
            outputs(1)


def kernel(**inputs):
    import numpy as np
    import concourse.bacc as bacc
    from concourse.bass_utils import run_bass_kernel_spmd

    a = {k: np.ascontiguousarray(v) for k, v in inputs.items()}

    def up_layout(rows):
        return rows.reshape(-1, P, KD, P).transpose(0, 3, 2, 1).reshape(-1, P, D)

    def padded(rows):
        return np.concatenate([rows, np.zeros((SHC * P - rows.shape[0], rows.shape[1]), rows.dtype)])

    gu = a["L1_ffn_shared_gate_up"]
    down = padded(a["L1_ffn_shared_down"].T).reshape(SHC, P, D)
    arrays = {
        "x": a["x"],
        "ctx": a["ctx_2048"],
        "ctx_t": a["ctx_2048"].reshape(B, S, KD, P).transpose(3, 0, 2, 1),
        "mask": a["mask_BxS2_bk0"],
        "g_xattn": a["g_xattn"],
        "g_ffn": a["g_ffn"],
        "gate0": a["L0_ffn_gate_w"].reshape(KD, P, E0).transpose(1, 0, 2),
        "gate0_b": a["L0_ffn_gate_b"],
        "w0": np.concatenate([up_layout(a["L0_ffn_w1"].transpose(0, 2, 1).reshape(E0 * F0, D)),
                              a["L0_ffn_w2"].reshape(-1, P, D)], axis=2),
        "b1": a["L0_ffn_b1"].reshape(-1, P).T,
        "b2": a["L0_ffn_b2"],
        "gate1": a["L1_ffn_gate_w"].reshape(E1, KD, P).transpose(2, 1, 0),
        "w1": np.concatenate([up_layout(a["L1_ffn_experts_w1"].reshape(E1 * I1, D)),
                              a["L1_ffn_experts_w2"].transpose(0, 2, 1).reshape(-1, P, D)], axis=2),
        "w_shared": np.concatenate([np.concatenate([up_layout(padded(gu[:SH1])), down], axis=2),
                                    np.concatenate([up_layout(padded(gu[SH1:])), np.zeros_like(down)], axis=2)]),
    }
    nc = bacc.Bacc("TRN2", target_bir_lowering=False, num_devices=1)
    args = {}
    for name, v in arrays.items():
        arrays[name] = v = np.ascontiguousarray(v)
        args[name] = nc.dram_tensor(f"in_{name}", v.shape, mybir.dt.from_np(v.dtype), kind="ExternalInput").ap()
    out = nc.dram_tensor("out_x", (B, S, D), F32, kind="ExternalOutput").ap()
    flamingo_kernel(nc, **args, out=out)
    r = run_bass_kernel_spmd(nc, [{f"in_{k}": v for k, v in arrays.items()}], core_ids=[0])
    return r.results[0]["out_x"]
```

```python
import concourse.bass as bass
from concourse import mybir
from contextlib import ExitStack

F32 = mybir.dt.float32
F32R = mybir.dt.float32r
U8 = mybir.dt.uint8
ALU = mybir.AluOpType
ACT = mybir.ActivationFunctionType
AX_X = mybir.AxisListType.X

P = 128
B, S, D = 8, 128, 256
KD = D // P
TOK = B * S
HALF = TOK // 2
PAIRS = B // 2

E0, F0, TOP0 = 8, 1024, 2
E1, I1, TOP1, SH1 = 64, 176, 6, 352
EPS = 1e-5
NEG = -1e30

ROUNDS = 8
CH0 = F0 // P
EPR1 = E1 // ROUNDS
CH1 = EPR1 * I1 // P
SHC = -(-SH1 // P)
SLOTS = CH1
CSLOTS = 4
SPAN0 = CH0 // 2
UNIT = (2, 2, 1, 1)
DVE_FROM = (4, 6, 8, 8)
GROUPS_BEFORE = tuple(sum(B // u for u in UNIT[:n]) for n in range(4))
WARM = (12, 6, 8)
COMB_COL = (3 * E0, 0)
SMALL = 7
AHEAD = 2
STEPS0, STEPSH, STEPS1 = 2 * CH0 * ROUNDS, 2 * SHC, 2 * CH1 * ROUNDS
BASE_SH = STEPS0
BASE1 = STEPS0 + STEPSH
LAST = STEPS0 + STEPSH + STEPS1
WB_SH = CH0 * ROUNDS
WB1 = WB_SH + 2 * SHC
CREDIT = 2


def loads_before(layer, slot):
    if layer == 0:
        return 0
    return (ROUNDS if slot < CH0 else 0) + (1 if slot < 2 * SHC else 0)


def pieces(t):
    found, row = [], t * P
    while row < (t + 1) * P:
        expert = row // I1
        end = min((expert + 1) * I1, (t + 1) * P)
        found.append((expert, row - t * P, end - t * P))
        row = end
    return found


def spread_loads(slot, chunks):
    return sum(len(pieces(t)) for t in range(chunks) if t % CSLOTS == slot)


def flamingo_kernel(nc, x, ctx, ctx_t, mask, g_xattn, g_ffn, gate0, gate0_b, w0, b1, b2,
                    gate1, w1, w_shared, out):
    comb_rows = nc.dram_tensor("comb_rows", (2, E1, TOK), F32).ap()

    with ExitStack() as stack:
        def sb(name, shape, dt=F32):
            return stack.enter_context(nc.sbuf_tensor(name, shape, dt))

        def sem(name):
            return stack.enter_context(nc.semaphore(name))

        xs = sb("xs", [P, B, D])
        xn = sb("xn", [P, B, D])
        xn_t = sb("xn_t", [P, KD, TOK])
        xt_hi = sb("xt_hi", [P, KD, TOK], F32R)
        xt_lo = sb("xt_lo", [P, KD, TOK], F32R)
        ctx_sb = sb("ctx_sb", [P, B, D])
        ctx_tsb = sb("ctx_tsb", [P, B, KD, S])
        mask_sb = sb("mask_sb", [P, B, S], U8)
        ident = sb("ident", [P, P])
        gains = sb("gains", [P, 4])
        tanh_g = sb("tanh_g", [P, 4])
        valid = sb("valid", [P, B])
        row_max = sb("row_max", [P, B])
        neg_max = sb("neg_max", [P, B])
        row_sum = sb("row_sum", [P, B])
        row_inv = sb("row_inv", [P, B])
        row_gain = sb("row_gain", [P, B])
        stats = sb("stats", [P, B, 6])
        mean_var = sb("mean_var", [P, B, 2])
        rstd = sb("rstd", [P, B])
        shift_n = sb("shift_n", [P, B])
        gate_sb = [sb("gate0_sb", [P, KD, E0]), sb("gate1_sb", [P, KD, E1])]
        gate_b_sb = sb("gate_b_sb", [E0, 1])
        b1_sb = sb("b1_sb", [P, WB_SH])
        b1_round = sb("b1_round", [P, CH0])
        b2_sb = sb("b2_sb", [3 * E0, D])
        b2_hi = sb("b2_hi", [3 * E0, D], F32R)
        b2_lo = sb("b2_lo", [3 * E0, D], F32R)
        b2_up = sb("b2_up", [3 * E0, D])
        b2_low = sb("b2_low", [3 * E0, D])
        b2_stack = sb("b2_stack", [3 * E0, D], F32R)
        comb_stack = sb("comb_stack", [3 * E0, TOK], F32R)
        comb_hi = sb("comb_hi", [P, B, E0], F32R)
        middle = sb("middle", [3 * E0, 1])
        outer = sb("outer", [3 * E0, 1])
        stage = sb("stage", [P, SLOTS, 2 * D])
        w_hi = sb("w_hi", [P, SLOTS, 2 * D], F32R)
        w_lo = sb("w_lo", [P, SLOTS, 2 * D], F32R)
        hid_hi = sb("hid_hi", [P, 2, HALF], F32R)
        hid_lo = sb("hid_lo", [P, 2, HALF], F32R)
        y_t = sb("y_t", [P, KD, TOK])
        masked = y_t[:, 0, :].rearrange("p (b s) -> p b s", b=B)
        probs = y_t[:, 1, :].rearrange("p (b s) -> p b s", b=B)
        shared_act = y_t[:, 0, :].rearrange("p (h t) -> p h t", h=2)
        shared_hid = y_t[:, 1, :].rearrange("p (h t) -> p h t", h=2)
        probs_t = sb("probs_t", [P, B, S])
        score1 = sb("score1", [P, 2, 2 * D])
        logit = sb("logit", [P, B * E1])
        expo = sb("expo", [P, B * E1])
        pext = [sb("pext0", [P, B, E0 + 8 - TOP0]), sb("pext1", [P, B, E1 + 8 - TOP1])]
        prep = [sb("prep0", [P, B, E0 + 8 - TOP0]), sb("prep1", [P, B, E1 + 8 - TOP1])]
        top8 = sb("top8", [P, B, 8])
        comb = sb("comb", [P, B, E1])
        comb_t = sb("comb_t", [E1, TOK])
        logit_t = comb_t[0:E0, :]
        comb_b = sb("comb_b", [P, CSLOTS, TOK])
        zero = sb("zero", [P, 1])
        minus_half = sb("minus_half", [P, 2])
        scratch = sb("scratch", [P, 4])

        ps_h = [stack.enter_context(nc.psum_tensor(f"ps_h{i}", [P, HALF], F32)) for i in range(2)]
        ps_a = [stack.enter_context(nc.psum_tensor(f"ps_a{i}", [P, HALF], F32)) for i in range(2)]
        ps_o = [stack.enter_context(nc.psum_tensor(f"ps_o{i}", [P, HALF], F32)) for i in range(4)]
        ps_r = [ps_o[2], ps_o[3], ps_h[0], ps_h[1], ps_a[0], ps_a[1], ps_o[2], ps_o[3]]
        ps_t = ps_h + ps_a

        def shared_banks(s):
            return ps_a if s == 1 else ps_h

        x_in = [sem(f"x_in{q}") for q in range(PAIRS)]
        ctx_t_in = [sem(f"ctx_t_in{q}") for q in range(PAIRS)]
        ctx_in, mask_in, gains_in, small_in = (sem(n) for n in ("ctx_in", "mask_in", "gains_in", "small_in"))
        const_ready = sem("const_ready")
        vec = sem("vec")
        gains_ready, moments_ready, rstd_ready, scale_ready, xn_ready, xn_ready_dve = (
            sem(n) for n in ("gains_ready", "moments_ready", "rstd_ready", "scale_ready", "xn_ready", "xn_ready_dve"))
        xn_turned, xt_hi_ready = sem("xn_turned"), sem("xt_hi_ready")
        xn_t_ready_act, xn_t_ready_dve = sem("xn_t_ready_act"), sem("xn_t_ready_dve")
        xt_lo_ready = [sem("xt_lo_dve_ready"), sem("xt_lo_pool_ready")]
        score0_ready, max_ready, probs_ready, probs_turned, probs_t_ready, read0_ready = (
            sem(n) for n in ("score0_ready", "max_ready", "probs_ready", "probs_turned", "probs_t_ready", "read0_ready"))
        score1_done, score1_ready, read1_ready = (sem(n) for n in ("score1_done", "score1_ready", "read1_ready"))
        logits_done, shifted_ready, expo_ready, comb_ready, comb_turned, comb_t_ready, comb_out = (
            sem(n) for n in ("logits_done", "shifted_ready", "expo_ready", "comb_ready", "comb_turned", "comb_t_ready",
                             "comb_out"))
        w_in = [sem(f"w_in{t}") for t in range(SLOTS)]
        w_split = sem("w_split")
        comb_in = [sem(f"comb_in{c}") for c in range(CSLOTS)]
        up_done, linear_done, act_done, mult_done, hi_done, lo_done, down_done = (
            sem(n) for n in ("up_done", "linear_done", "act_done", "mult_done", "hi_done", "lo_done", "down_done"))
        y_ready_act, y_ready_dve, y_turned, out_ready, stored = (
            sem(n) for n in ("y_ready_act", "y_ready_dve", "y_turned", "out_ready", "stored"))
        comb_split, b2_split, stacks_ready = (sem(n) for n in ("comb_split", "b2_split", "stacks_ready"))
        split_hi, bias_ready = sem("split_hi"), sem("bias_ready")
        gated, logit_t_ready = sem("gated"), sem("logit_t_ready")
        first_turned, first_spread_dve, first_spread_act = (
            sem(n) for n in ("first_turned", "first_spread_dve", "first_spread_act"))

        def wait_normed(engine, n, b):
            if b >= DVE_FROM[n]:
                engine.wait_ge(xn_ready_dve, sum(B - f for f in DVE_FROM[:n]) + b - DVE_FROM[n] + 1)
            else:
                engine.wait_ge(xn_ready, sum(DVE_FROM[:n]) + b + 1)

        def wait_turned(engine, n, q):
            if n == 0 or q < PAIRS // 2:
                engine.wait_ge(xn_t_ready_act, (0, PAIRS, PAIRS + PAIRS // 2)[n] + q + 1)
            else:
                engine.wait_ge(xn_t_ready_dve, PAIRS // 2 * (n - 2) + q + 1)

        block = stack.enter_context(nc.Block())

        @block.sync
        def _(sp):
            for q in range(PAIRS):
                sp.dma_start(xs[:, 2 * q:2 * q + 2, :], x[2 * q:2 * q + 2].rearrange("b s d -> s b d")
                             ).then_inc(x_in[q], 16)
            for q in range(PAIRS):
                sp.dma_start(ctx_tsb[:, 2 * q:2 * q + 2], ctx_t[:, 2 * q:2 * q + 2]).then_inc(ctx_t_in[q], 16)
            sp.dma_start(ctx_sb[:], ctx.rearrange("b s d -> s b d")).then_inc(ctx_in, 16)
            for dst, src in ((gate_sb[0][:], gate0), (gate_sb[1][:], gate1), (gate_b_sb[:], gate0_b.unsqueeze(1)),
                             (b1_sb[:], b1), *((b2_sb[j * E0:(j + 1) * E0, :], b2) for j in range(3))):
                sp.dma_start(dst, src).then_inc(small_in, 16)

            def load_weights(block, t, split_no):
                if split_no is not None:
                    sp.wait_ge(w_split, split_no)
                sp.dma_start(stage[:, t, :], block).then_inc(w_in[t], 16)

            def spread0(i, part, steps_done):
                if steps_done is not None:
                    sp.wait_ge(mult_done, steps_done)
                sp.dma_start(comb_b[:, part, :], comb_rows[0, i].partition_broadcast(P)).then_inc(comb_in[part], 16)

            def spread1(i, t, steps_done):
                if steps_done is not None:
                    sp.wait_ge(mult_done, steps_done)
                for expert, first, end in pieces(t):
                    sp.dma_start(comb_b[first:end, t % CSLOTS, :],
                                 comb_rows1[i, expert].partition_broadcast(end - first)
                                 ).then_inc(comb_in[t % CSLOTS], 16)

            def round0(i, first, last):
                for t in range(CH0):
                    if t % SPAN0 == 0 and not (first and t == 0):
                        spread0(i, t // SPAN0, None if first else
                                (i - 1) * (2 * CH0) + (2 * (t + SPAN0) + CREDIT))
                    if not last:
                        load_weights(w0_v[i + 1, t], t, i * CH0 + (t + 1))
                    elif t < 2 * SHC:
                        load_weights(w_shared[t], t, i * CH0 + (t + 1))
                    else:
                        load_weights(w1_v[0, t], t, i * CH0 + (t + 1))

            def round1(i, first, last):
                for t in range(CH1):
                    if t >= CSLOTS:
                        free = i * (2 * CH1) + (BASE1 + 2 * (t - CSLOTS + 1) + CREDIT)
                    elif first:
                        free = STEPS0 + CREDIT
                    else:
                        before = max(u for u in range(CH1) if u % CSLOTS == t)
                        free = (i - 1) * (2 * CH1) + (BASE1 + 2 * (before + 1) + CREDIT)
                    if not (first and t == 0):
                        spread1(i, t, free)
                    if not last:
                        load_weights(w1_v[i + 1, t], t, i * CH1 + (WB1 + t + 1))

            def send_comb(layer):
                experts = (E0, E1)[layer]
                sp.wait_ge(comb_t_ready, 2 * (layer + 1))
                first = COMB_COL[layer]
                sp.dma_start(comb_rows[layer, 0:experts, :], comb_t[first:first + experts, :]).then_inc(comb_out, 16)
                sp.wait_ge(comb_out, 16 * (layer + 1))

            w0_v = w0.rearrange("(i t) p n -> i t p n", t=CH0)
            w1_v = w1.rearrange("(i t) p n -> i t p n", t=CH1)
            comb_rows1 = comb_rows[1].rearrange("(i e) t -> i e t", e=EPR1)
            for t in range(CH0):
                load_weights(w0_v[0, t], t, None)
            for t in range(CH0, CH1):
                load_weights(w1_v[0, t], t, None)
            send_comb(0)
            round0(0, True, False)
            with sp.Fori(1, ROUNDS - 1) as i:
                round0(i, False, False)
            round0(ROUNDS - 1, False, True)
            for t in range(2 * SHC):
                load_weights(w1_v[0, t], t, WB_SH + t + 1)
            send_comb(1)
            round1(0, True, False)
            with sp.Fori(1, ROUNDS - 1) as i:
                round1(i, False, False)
            round1(ROUNDS - 1, False, True)
            for q in range(PAIRS):
                sp.wait_ge(out_ready, q + 1)
                sp.dma_start(out[2 * q:2 * q + 2].rearrange("b s d -> s b d"), xs[:, 2 * q:2 * q + 2, :]
                             ).then_inc(stored, 16)
            sp.wait_ge(stored, 16 * PAIRS)

        @block.gpsimd
        def _(pool):
            pool.memset(zero[:], 0.0).then_inc(const_ready, 1)
            pool.memset(ident[:], 0.0).then_inc(const_ready, 1)
            pool.memset(minus_half[:], -0.5).then_inc(const_ready, 1)
            pool.wait_ge(const_ready, 3)
            pool.affine_select(out=ident[:], in_=ident[:], compare_op=ALU.not_equal, fill=1.0, base=0,
                               pattern=[[-1, P]], channel_multiplier=1).then_inc(const_ready, 1)
            pool.memset(scratch[:, 0:1], 0.0).then_inc(act_done, CREDIT)
            pool.memset(scratch[:, 1:2], 0.0).then_inc(mult_done, CREDIT)
            pool.memset(scratch[:, 2:3], 0.0).then_inc(down_done, CREDIT)
            pool.memset(scratch[:, 3:4], 0.0).then_inc(lo_done, CREDIT)

            def split(t, loads, block_no, free_after):
                pool.wait_ge(w_in[t], 16 * loads)
                if free_after is not None:
                    pool.wait_ge(down_done, free_after)
                pool.tensor_tensor(w_hi[:, t, :], stage[:, t, :], zero[:].broadcast_to([P, 2 * D]), ALU.add
                                   ).then_inc(split_hi, 1)
                pool.wait_ge(split_hi, block_no + 1)
                pool.tensor_tensor(w_lo[:, t, :], stage[:, t, :], w_hi[:, t, :].bitcast(F32), ALU.subtract
                                   ).then_inc(w_split, 1)

            def stack_biases():
                def then(ins, steps):
                    ins.then_inc(b2_split, 1)
                    pool.wait_ge(b2_split, steps)

                rows = [3 * E0, D]
                pool.wait_ge(small_in, 16 * SMALL)
                then(pool.memset(middle[:], 1.0), 1)
                then(pool.affine_select(out=middle[:], in_=middle[:], compare_op=ALU.is_ge, fill=0.0, base=-E0,
                                        pattern=[[0, 1]], channel_multiplier=1), 2)
                then(pool.affine_select(out=middle[:], in_=middle[:], compare_op=ALU.is_ge, fill=0.0,
                                        base=2 * E0 - 1, pattern=[[0, 1]], channel_multiplier=-1), 3)
                then(pool.memset(outer[:], 1.0), 4)
                then(pool.tensor_tensor(outer[:], outer[:], middle[:], ALU.subtract), 5)
                then(pool.tensor_tensor(b2_hi[:], b2_sb[:], zero[0:3 * E0].broadcast_to(rows), ALU.add), 6)
                then(pool.tensor_tensor(b2_lo[:], b2_sb[:], b2_hi[:].bitcast(F32), ALU.subtract), 7)
                then(pool.tensor_tensor(b2_up[:], b2_hi[:].bitcast(F32), outer[:].broadcast_to(rows), ALU.mult), 8)
                then(pool.tensor_tensor(b2_low[:], b2_lo[:].bitcast(F32), middle[:].broadcast_to(rows), ALU.mult), 9)
                pool.tensor_tensor(b2_stack[:], b2_up[:], b2_low[:], ALU.add).then_inc(stacks_ready, 1)
                pool.wait_ge(comb_t_ready, 2)
                pool.tensor_tensor(comb_stack[:], comb_t[0:3 * E0, :], zero[0:3 * E0].broadcast_to([3 * E0, TOK]),
                                   ALU.add).then_inc(stacks_ready, 1)

            def after_step(step):
                return step + 1 + CREDIT

            def lower_norm(n, q):
                pool.wait_ge(xt_hi_ready, PAIRS * n + q + 1)
                cols = slice(q * 2 * S, (q + 1) * 2 * S)
                pool.tensor_tensor(xt_lo[:, :, cols], xn_t[:, :, cols], xt_hi[:, :, cols].bitcast(F32),
                                   ALU.subtract).then_inc(xt_lo_ready[1], 1)

            def scales(n, q):
                part = slice(UNIT[n] * q, UNIT[n] * (q + 1))
                pool.wait_ge(moments_ready, GROUPS_BEFORE[n] + q + 1)
                pool.tensor_tensor(rstd[:, part], mean_var[:, part, 1], minus_half[:, 0:UNIT[n]], ALU.pow
                                   ).then_inc(rstd_ready, 1)
                pool.wait_ge(rstd_ready, GROUPS_BEFORE[n] + q + 1)
                pool.tensor_tensor(shift_n[:, part], mean_var[:, part, 0], rstd[:, part], ALU.mult
                                   ).then_inc(scale_ready, 1)

            for q in range(PAIRS):
                scales(0, q)
            for t in range(AHEAD):
                split(t, 1, t, None)
            for q in range(PAIRS):
                scales(1, q)
            for q in range(PAIRS // 2, PAIRS):
                lower_norm(0, q)
            for t in range(AHEAD, CH0):
                split(t, 1, t, None)
            stack_biases()
            with pool.Fori(1, ROUNDS) as i:
                for t in range(CH0):
                    split(t, i + 1, i * CH0 + t, (i - 1) * (2 * CH0) + after_step(2 * t + 1))
            for j in range(2 * SHC):
                split(j, ROUNDS + 1, WB_SH + j, after_step(2 * ((ROUNDS - 1) * CH0 + j) + 1))
            for n in (2, 3):
                for q in range(B // UNIT[n]):
                    scales(n, q)
            for q in range(PAIRS // 2, PAIRS):
                lower_norm(1, q)
            for t in range(CH1):
                if t < 2 * SHC:
                    free = after_step(BASE_SH + 2 * (t % SHC) + 1)
                elif t < CH0:
                    free = after_step(2 * ((ROUNDS - 1) * CH0 + t) + 1)
                else:
                    free = None
                split(t, loads_before(1, t) + 1, WB1 + t, free)
            with pool.Fori(1, ROUNDS) as i:
                for t in range(CH1):
                    split(t, i + (loads_before(1, t) + 1), i * CH1 + (WB1 + t),
                          (i - 1) * (2 * CH1) + after_step(BASE1 + 2 * t + 1))

        @block.tensor
        def _(pe):
            def keep_warm(times, bank):
                for _ in range(times):
                    nc.tensor.matmul(bank[:, 0:P], ident[:], ident[:], start=True, stop=True)

            def turn_norm(n, q):
                for b in (2 * q, 2 * q + 1):
                    wait_normed(pe, (0, 1, 3)[n], b)
                    for k in range(KD):
                        m = nc.tensor.transpose(ps_t[q][:, k * 2 * S + (b % 2) * S:k * 2 * S + (b % 2 + 1) * S],
                                                xn[:, b, k * P:(k + 1) * P], ident[:])
                m.then_inc(xn_turned, 1)

            def three(dst, w, w_cols, moving, m_cols, start, stop):
                (hi_w, lo_w), (hi_m, lo_m) = w, moving
                nc.tensor.matmul(dst, w_cols(hi_w), m_cols(hi_m), start=start, stop=False)
                nc.tensor.matmul(dst, w_cols(hi_w), m_cols(lo_m), start=False, stop=False)
                return nc.tensor.matmul(dst, w_cols(lo_w), m_cols(hi_m), start=False, stop=stop)

            def up(dst, t, half, first_col):
                for k in range(KD):
                    m = three(dst, (w_hi, w_lo), lambda w: w[:, t, first_col + k * P:first_col + (k + 1) * P],
                              (xt_hi, xt_lo), lambda v: v[:, k, half * HALF:(half + 1) * HALF], k == 0, k == KD - 1)
                return m

            def down(t, half, start, stop):
                for d in range(KD):
                    m = three(ps_o[2 * d + half][:], (w_hi, w_lo), lambda w: w[:, t, D + d * P:D + (d + 1) * P],
                              (hid_hi, hid_lo), lambda v: v[:, half, :], start, stop)
                m.then_inc(down_done, 1)

            def up_step(half, t, step, block_no):
                if half == 0:
                    pe.wait_ge(w_split, block_no + 1)
                pe.wait_ge(act_done, step + 1)
                up(ps_h[half][:], t, half, 0).then_inc(up_done, 1)

            def round_steps(layer, i, last, opens=False):
                chunks = CH0 if layer == 0 else CH1
                base = 0 if layer == 0 else BASE1
                wbase = 0 if layer == 0 else WB1
                steps = 2 * chunks
                for s in range(steps):
                    ahead = s + 2 + opens
                    wrap = ahead >= steps
                    t, half = (ahead % steps) // 2, s % 2
                    if not (last and wrap) and not (opens and s in (0, steps - 1)):
                        up_step(ahead % 2, t, i * steps + (base + ahead), i * chunks + (wbase + ahead // 2))
                    pe.wait_ge(lo_done, i * steps + (base + s + 1 + CREDIT))
                    down(s // 2, half, opens and s < 2, last and s >= steps - 2)

            def rounds(layer, first):
                with pe.Fori(first, ROUNDS - 1) as i:
                    round_steps(layer, i, False)
                round_steps(layer, ROUNDS - 1, True)

            def gate0_pair(q):
                wait_turned(pe, 1, q)
                for k in range(KD):
                    m = nc.tensor.matmul(ps_o[q // 2][0:E0, (q % 2) * 2 * S:(q % 2 + 1) * 2 * S], gate_sb[0][:, k, :],
                                         xn_t[:, k, q * 2 * S:(q + 1) * 2 * S], start=(k == 0), stop=(k == KD - 1))
                if q % 2:
                    m.then_inc(gated, 1)

            def turn_probs(q):
                for b in (2 * q, 2 * q + 1):
                    pe.wait_ge(probs_ready, b + 1)
                    m = nc.tensor.transpose(ps_o[q][:, (b % 2) * S:(b % 2 + 1) * S], probs[:, b, :], ident[:])
                m.then_inc(probs_turned, 1)

            def read0(q):
                pe.wait_ge(probs_t_ready, q + 1)
                for b in (2 * q, 2 * q + 1):
                    m = nc.tensor.matmul(ps_t[q][:, (b % 2) * D:(b % 2 + 1) * D], probs_t[:, b, :], ctx_sb[:, b, :],
                                         start=True, stop=True)
                m.then_inc(read0_ready, 1)

            def turn_logits():
                pe.wait_ge(logit_t_ready, 2)
                for b in range(B):
                    m = nc.tensor.transpose(ps_o[2][:, b * E0:(b + 1) * E0], logit_t[:, b * S:(b + 1) * S],
                                            ident[0:E0, 0:E0])
                m.then_inc(logits_done, 1)

            def gate1_pair(q):
                wait_turned(pe, 2, q)
                for b in (2 * q, 2 * q + 1):
                    for k in range(KD):
                        m = nc.tensor.matmul(ps_o[0][:, b * E1:(b + 1) * E1], xn_t[:, k, b * S:(b + 1) * S],
                                             gate_sb[1][:, k, :], start=(k == 0), stop=(k == KD - 1))
                if q == PAIRS - 1:
                    m.then_inc(logits_done, 1)

            def score0(q):
                pe.wait_ge(ctx_t_in[q], 16)
                wait_turned(pe, 0, q)
                for b in (2 * q, 2 * q + 1):
                    for k in range(KD):
                        m = nc.tensor.matmul(ps_o[q][:, (b % 2) * S:(b % 2 + 1) * S], xn_t[:, k, b * S:(b + 1) * S],
                                             ctx_tsb[:, b, k, :], start=(k == 0), stop=(k == KD - 1))
                m.then_inc(score0_ready, 1)

            def turn_first(layer, half, bank):
                pe.wait_ge(comb_ready, layer + 1)
                for b in range(4 * half, 4 * half + 4):
                    column = comb[:, b, COMB_COL[layer]:COMB_COL[layer] + 1]
                    m = nc.tensor.matmul(bank[:, (b % 4) * S:(b % 4 + 1) * S], column.broadcast_to([P, P]), ident[:],
                                         start=True, stop=True)
                m.then_inc(first_turned, 1)

            def turn_comb(layer, banks):
                rows = (4 * E0, E1)[layer]
                pe.wait_ge(comb_ready, layer + 1)
                if layer == 0:
                    pe.wait_ge(comb_split, 3)
                for b in range(B):
                    m = nc.tensor.transpose(banks[b // 4][0:rows, (b % 4) * S:(b % 4 + 1) * S],
                                            comb[:, b, 0:rows], ident[:])
                m.then_inc(comb_turned, 1)

            def read1(b):
                pe.wait_ge(score1_ready, b + 1)
                if 2 <= b < 6:
                    wait_normed(pe, 2, 2 * (b - 2) + 1)
                elif b >= 6:
                    wait_normed(pe, 3, b - 6)
                for k in range(KD):
                    m = nc.tensor.matmul(ps_r[b][:, 0:D], ctx_tsb[:, b, k, :],
                                         score1[:, b % 2, k * D:(k + 1) * D], start=(k == 0), stop=(k == KD - 1))
                m.then_inc(read1_ready, 1)

            def turn_output(layer):
                for b in range(B):
                    if b % (B // 2) == 0:
                        pe.wait_ge(y_ready_act, 2 * layer + b // (B // 2) + 1)
                        pe.wait_ge(y_ready_dve, 2 * layer + b // (B // 2) + 1)
                    for d in range(KD):
                        m = nc.tensor.transpose(ps_t[b // 2][:, (b % 2) * D + d * P:(b % 2) * D + (d + 1) * P],
                                                y_t[:, d, b * S:(b + 1) * S], ident[:])
                    if b % 2:
                        m.then_inc(y_turned, 1)

            pe.wait_ge(const_ready, 4)
            keep_warm(WARM[0], ps_a[1])
            turn_norm(0, 0)
            turn_norm(0, 1)
            score0(0)
            turn_norm(0, 2)
            score0(1)
            turn_norm(0, 3)
            turn_probs(0)
            score0(2)
            pe.wait_ge(ctx_in, 16)
            read0(0)
            turn_probs(1)
            score0(3)
            read0(1)
            turn_probs(2)
            read0(2)
            turn_probs(3)
            read0(3)
            pe.wait_ge(small_in, 16 * SMALL)
            keep_warm(WARM[1], ps_o[0])
            turn_norm(1, 0)
            for q in range(1, PAIRS):
                turn_norm(1, q)
                gate0_pair(q - 1)
            gate0_pair(PAIRS - 1)
            turn_logits()
            for half in range(2):
                pe.wait_ge(xt_lo_ready[half], 2)
                up_step(half, 0, half, 0)
            up_step(0, 1, 2, 1)
            turn_first(0, 0, ps_o[0])
            turn_comb(0, (ps_o[1], ps_o[3]))
            turn_first(0, 1, ps_o[2])
            up_step(1, 1, 3, 1)
            pe.wait_ge(first_spread_dve, 1)
            pe.wait_ge(first_spread_act, 1)
            pe.wait_ge(comb_t_ready, 2)
            round_steps(0, 0, False, opens=True)
            pe.wait_ge(stacks_ready, 2)
            for d in range(KD):
                for half in range(2):
                    nc.tensor.matmul(ps_o[2 * d + half][:], b2_stack[:, d * P:(d + 1) * P],
                                     comb_stack[:, half * HALF:(half + 1) * HALF], start=False, stop=False)
            rounds(0, 1)
            turn_output(0)
            keep_warm(WARM[2], ps_o[2])
            for b in range(B):
                wait_normed(pe, 2, b)
                if b >= 2:
                    pe.wait_ge(score1_ready, b - 1)
                for k in range(KD):
                    m = nc.tensor.matmul(ps_o[b % 2][:, k * D:(k + 1) * D], xn[:, b, k * P:(k + 1) * P],
                                         ctx_sb[:, b, :], start=True, stop=True)
                m.then_inc(score1_done, 1)
                if b >= 1:
                    read1(b - 1)
            read1(B - 1)
            for q in range(PAIRS):
                wait_normed(pe, 3, q + 2)
                turn_norm(2, q)
                if q in (1, 2):
                    gate1_pair(q - 1)
            gate1_pair(2)
            for s in range(STEPSH):
                if s < 2:
                    pe.wait_ge(xt_lo_ready[s], 4)
                if s % 2 == 0:
                    pe.wait_ge(w_split, WB_SH + s // 2 + 1)
                before = 0 if s == 2 else s - 1
                if s >= 2:
                    pe.wait_ge(act_done, BASE_SH + before + 1 + CREDIT)
                up(shared_banks(s)[0][:], s // 2, s % 2, 0).then_inc(up_done, 1)
                if s % 2 == 0:
                    pe.wait_ge(w_split, WB_SH + SHC + s // 2 + 1)
                if s >= 2:
                    pe.wait_ge(mult_done, BASE_SH + before + 1 + CREDIT)
                up(shared_banks(s)[1][:], SHC + s // 2, s % 2, 0).then_inc(linear_done, 1)
                if s == 0:
                    gate1_pair(3)
                if s == 5:
                    pe.wait_ge(first_spread_dve, 2)
                    pe.wait_ge(first_spread_act, 2)
                    turn_comb(1, ps_a)
                if s >= 1:
                    pe.wait_ge(lo_done, BASE_SH + s + CREDIT)
                    if s == 1:
                        pe.wait_ge(shifted_ready, 2)
                    down((s - 1) // 2, (s - 1) % 2, s < 3, False)
                if s == 4:
                    for half in range(2):
                        turn_first(1, half, ps_a[half])
            pe.wait_ge(act_done, BASE1 + CREDIT)
            up_step(0, 0, BASE1, WB1)
            pe.wait_ge(mult_done, BASE1 + CREDIT)
            up_step(1, 0, BASE1 + 1, WB1)
            pe.wait_ge(lo_done, BASE1 + CREDIT)
            down(SHC - 1, 1, False, False)
            rounds(1, 0)
            turn_output(1)

        @block.scalar
        def _(act):
            def norm(n, q):
                act.wait_ge(scale_ready, GROUPS_BEFORE[n] + q + 1)
                for b in range(UNIT[n] * q, UNIT[n] * (q + 1)):
                    nc.scalar.activation(xn[:, b, :], xs[:, b, :], ACT.Identity, bias=shift_n[:, b:b + 1],
                                         scale=rstd[:, b:b + 1]).then_inc(xn_ready, 1)

            def take_turned(n, q):
                act.wait_ge(xn_turned, PAIRS * n + q + 1)
                nc.scalar.activation(xn_t[:, :, q * 2 * S:(q + 1) * 2 * S],
                                     ps_t[q][:].rearrange("p (k t) -> p k t", k=KD), ACT.Copy).then_inc(xn_t_ready_act, 1)

            def upper_norm(n, q):
                wait_turned(act, n, q)
                nc.scalar.activation(xt_hi[:, :, q * 2 * S:(q + 1) * 2 * S],
                                     xn_t[:, :, q * 2 * S:(q + 1) * 2 * S], ACT.Copy).then_inc(xt_hi_ready, 1)

            def take_logits(half):
                act.wait_ge(gated, half + 1)
                nc.scalar.activation(logit_t[:, half * HALF:(half + 1) * HALF], ps_o[half][0:E0, :], ACT.Identity,
                                     bias=gate_b_sb[:]).then_inc(logit_t_ready, 1)

            def spread_first(layer, bank):
                act.wait_ge(first_turned, 2 * layer + 2)
                nc.scalar.activation(comb_b[:, 0, HALF:TOK], bank[:], ACT.Copy).then_inc(first_spread_act, 1)

            def exponent(layer):
                act.wait_ge(shifted_ready, layer + 1)
                n = B * (E0, E1)[layer]
                nc.scalar.activation(expo[:, 0:n], logit[:, 0:n], ACT.Exp).then_inc(expo_ready, 1)

            def take_comb(layer, banks, halves=(0, 1)):
                rows = (4 * E0, E1)[layer]
                act.wait_ge(comb_turned, layer + 1)
                for g in halves:
                    nc.scalar.activation(comb_t[0:rows, g * HALF:(g + 1) * HALF], banks[g][0:rows, :], ACT.Copy
                                         ).then_inc(comb_t_ready, 1)

            def upper_half(half, step_no, hidden):
                act.wait_ge(mult_done, step_no + 1 + CREDIT)
                act.wait_ge(down_done, step_no + 1)
                nc.scalar.activation(hid_hi[:, half, :], hidden, ACT.Copy).then_inc(hi_done, 1)

            def activate(half, step_no, func, bias):
                act.wait_ge(up_done, step_no + 1)
                act.wait_ge(lo_done, step_no + 1)
                nc.scalar.activation(ps_a[half][:], ps_h[half][:], func, bias=bias).then_inc(act_done, 1)

            def step(half, step_no, func, bias):
                activate(half, step_no, func, bias)
                upper_half(half, step_no, ps_a[half][:])

            def shared_step(half, step_no, banks):
                act.wait_ge(up_done, step_no + 1)
                act.wait_ge(lo_done, step_no + 1)
                nc.scalar.activation(shared_act[:, half, :], banks[0][:], ACT.Silu).then_inc(act_done, 1)
                upper_half(half, step_no, shared_hid[:, half, :])

            def outputs(layer):
                for half in range(2):
                    act.wait_ge(down_done, (STEPS0, LAST)[layer] - 1 + half + CREDIT)
                    nc.scalar.activation(y_t[:, 0, half * HALF:(half + 1) * HALF], ps_o[half][:], ACT.Copy,
                                         scale=tanh_g[:, 2 + layer:3 + layer]).then_inc(y_ready_act, 1)

            act.dma_start(mask_sb[:], mask.partition_broadcast(P)).then_inc(mask_in, 16)
            act.dma_start(gains[:, 0:2], g_xattn.partition_broadcast(P)).then_inc(gains_in, 16)
            act.dma_start(gains[:, 2:4], g_ffn.partition_broadcast(P)).then_inc(gains_in, 16)
            nc.scalar.preload_act_table(ACT.Exp)
            def exponents0(q):
                act.wait_ge(max_ready, q + 1)
                for b in (2 * q, 2 * q + 1):
                    nc.scalar.activation(probs[:, b, :], masked[:, b, :], ACT.Exp, bias=neg_max[:, b:b + 1],
                                         scale=float(D) ** -0.5, accum_out=row_sum[:, b:b + 1]).then_inc(probs_ready, 1)

            def take_probs(q):
                act.wait_ge(probs_turned, q + 1)
                nc.scalar.activation(probs_t[:, 2 * q:2 * q + 2, :].rearrange("p b s -> p (b s)"), ps_o[q][:, 0:2 * S],
                                     ACT.Copy).then_inc(probs_t_ready, 1)

            norm(0, 0)
            norm(0, 1)
            take_turned(0, 0)
            take_turned(0, 1)
            act.wait_ge(gains_in, 32)
            nc.scalar.activation(tanh_g[:], gains[:], ACT.Tanh).then_inc(gains_ready, 1)
            take_turned(0, 2)
            exponents0(0)
            take_turned(0, 3)
            take_probs(0)
            exponents0(1)
            take_probs(1)
            exponents0(2)
            take_probs(2)
            exponents0(3)
            take_probs(3)
            norm(1, 0)
            take_turned(1, 0)
            norm(1, 1)
            take_turned(1, 1)
            norm(1, 2)
            upper_norm(1, 0)
            upper_norm(1, 1)
            act.wait_ge(small_in, 16 * SMALL)
            take_logits(0)
            upper_norm(1, 2)
            upper_norm(1, 3)
            take_logits(1)
            exponent(0)
            nc.scalar.preload_act_table(ACT.Gelu_apprx_tanh)
            nc.scalar.activation(b1_round[:], b1_sb[:, 0:CH0], ACT.Copy).then_inc(bias_ready, 1)
            act.wait_ge(bias_ready, 1)
            for s in range(2):
                activate(s % 2, s, ACT.Gelu_apprx_tanh, b1_round[:, s // 2:s // 2 + 1])
            take_comb(0, (ps_o[1], ps_o[3]), (0,))
            upper_half(0, 0, ps_a[0][:])
            take_comb(0, (ps_o[1], ps_o[3]), (1,))
            spread_first(0, ps_o[2])
            for s in range(1, 2 * CH0 - 1):
                activate((s + 1) % 2, s + 1, ACT.Gelu_apprx_tanh, b1_round[:, (s + 1) // 2:(s + 1) // 2 + 1])
                upper_half(s % 2, s, ps_a[s % 2][:])
            upper_half(1, 2 * CH0 - 1, ps_a[1][:])
            with act.Fori(1, ROUNDS) as i:
                nc.scalar.activation(b1_round[:], b1_sb[:, bass.ds(i * CH0, CH0)], ACT.Copy).then_inc(bias_ready, 1)
                act.wait_ge(bias_ready, i + 1)
                for s in range(2 * CH0):
                    step(s % 2, i * (2 * CH0) + s, ACT.Gelu_apprx_tanh, b1_round[:, s // 2:s // 2 + 1])
            nc.scalar.preload_act_table(ACT.Sigmoid)
            outputs(0)

            def weigh(b):
                act.wait_ge(score1_done, b + 1)
                if b >= 2:
                    act.wait_ge(read1_ready, b - 1)
                nc.scalar.activation(score1[:, b % 2, :], ps_o[b % 2][:], ACT.Sigmoid, scale=float(S) ** -0.5
                                     ).then_inc(score1_ready, 1)

            norm(2, 0)
            norm(2, 1)
            weigh(0)
            norm(2, 2)
            norm(2, 3)
            weigh(1)
            norm(2, 4)
            norm(2, 5)
            weigh(2)
            norm(2, 6)
            norm(2, 7)
            weigh(3)
            weigh(4)
            norm(3, 0)
            weigh(5)
            norm(3, 1)
            weigh(6)
            norm(3, 2)
            weigh(7)
            for b in range(3, B):
                norm(3, b)
                if b == 5:
                    take_turned(2, 0)
                    take_turned(2, 1)
                if b == 6:
                    upper_norm(2, 0)
            for q in range(1, PAIRS):
                upper_norm(2, q)
            nc.scalar.preload_act_table(ACT.Silu)
            for s in range(STEPSH):
                shared_step(s % 2, BASE_SH + s, shared_banks(s))
                if s == 1:
                    exponent(1)
                    nc.scalar.preload_act_table(ACT.Silu)
                if s == 4:
                    spread_first(1, ps_a[1])
            take_comb(1, ps_a)
            act.wait_ge(comb_t_ready, 4)
            with act.Fori(0, ROUNDS) as i:
                for s in range(2 * CH1):
                    step(s % 2, i * (2 * CH1) + (BASE1 + s), ACT.Silu, 0.0)
            outputs(1)

        @block.vector
        def _(dve):
            count, gain_no = [0], [0]

            def link(ins):
                count[0] += 1
                ins.then_inc(vec, 1)
                dve.wait_ge(vec, count[0])

            def mark(ins):
                count[0] += 1
                ins.then_inc(vec, 1)
                return count[0]

            def layernorm(n, new_rows, lag):
                unit, groups = UNIT[n], B // UNIT[n]
                rows, stat, moment = {}, {}, {}

                def renew(q):
                    rows[q] = new_rows(q)

                def statistics(q):
                    if rows[q] is not None:
                        dve.wait_ge(vec, rows[q])
                    for b in range(unit * q, unit * (q + 1)):
                        m = nc.vector.bn_stats(stats[:, b, :], xs[:, b, :])
                    stat[q] = mark(m)

                def aggregate(q):
                    dve.wait_ge(vec, stat[q])
                    for b in range(unit * q, unit * (q + 1)):
                        m = nc.vector.bn_aggr(mean_var[:, b, :], stats[:, b, :])
                    moment[q] = mark(m)

                def moments(q):
                    part = slice(unit * q, unit * (q + 1))
                    dve.wait_ge(vec, moment[q])
                    nc.vector.tensor_scalar(mean_var[:, part, 1], mean_var[:, part, 1], EPS, None, ALU.add)
                    nc.vector.tensor_scalar(mean_var[:, part, 0], mean_var[:, part, 0], -1.0, None, ALU.mult
                                            ).then_inc(moments_ready, 1)

                if lag:
                    for q in range(groups + 1):
                        if q < groups:
                            renew(q)
                        if q > 0:
                            aggregate(q - 1)
                        if q < groups:
                            statistics(q)
                        if q > 0:
                            moments(q - 1)
                else:
                    for q in range(groups):
                        renew(q)
                        statistics(q)
                        aggregate(q)
                        moments(q)

            def over(v, n):
                return v.unsqueeze(2).broadcast_to([P, B, n])

            def routed(v, layer):
                return v[:, 0:B * (E0, E1)[layer]].rearrange("p (b e) -> p b e", b=B)

            def take_turned(n, q):
                dve.wait_ge(xn_turned, PAIRS * n + q + 1)
                nc.vector.tensor_copy(xn_t[:, :, q * 2 * S:(q + 1) * 2 * S],
                                      ps_t[q][:].rearrange("p (k t) -> p k t", k=KD)).then_inc(xn_t_ready_dve, 1)

            def lower_norm(n, q):
                dve.wait_ge(xt_hi_ready, PAIRS * (n - 1) + q + 1)
                cols = slice(q * 2 * S, (q + 1) * 2 * S)
                nc.vector.tensor_tensor(xt_lo[:, :, cols], xn_t[:, :, cols], xt_hi[:, :, cols].bitcast(F32),
                                        ALU.subtract).then_inc(xt_lo_ready[0], 1)

            def shift(layer, bank):
                experts = (E0, E1)[layer]
                lg, raw = routed(logit, layer), routed(bank, layer)
                dve.wait_ge(logits_done, layer + 1)
                link(nc.vector.tensor_reduce(row_max[:], raw, AX_X, ALU.max))
                nc.vector.tensor_tensor(lg, raw, over(row_max[:], experts), ALU.subtract).then_inc(shifted_ready, 1)

            def probabilities(layer):
                experts = (E0, E1)[layer]
                ex = routed(expo, layer)
                dve.wait_ge(expo_ready, layer + 1)
                link(nc.vector.tensor_reduce(row_sum[:], ex, AX_X, ALU.add))
                link(nc.vector.reciprocal(row_inv[:], row_sum[:]))
                link(nc.vector.tensor_tensor(pext[layer][:, :, 0:experts], ex, over(row_inv[:], experts), ALU.mult))

            def largest(layer):
                experts, top = ((E0, TOP0), (E1, TOP1))[layer]
                for b in range(B):
                    m = nc.vector.max(top8[:, b, :], pext[layer][:, b, 0:experts])
                link(m)
                link(nc.vector.memset(top8[:, :, top:8], -1.0))

            def take_out(layer):
                for b in range(B):
                    m = nc.vector.match_replace(prep[layer][:, b, :], top8[:, b, :], pext[layer][:, b, :], 0.0)
                link(m)

            def spread_first(layer, bank):
                dve.wait_ge(first_turned, 2 * layer + 1)
                nc.vector.tensor_copy(comb_b[:, 0, 0:HALF], bank[:]).then_inc(first_spread_dve, 1)

            def combine(layer):
                experts, top = ((E0, TOP0), (E1, TOP1))[layer]
                ex = routed(expo, layer)
                link(nc.vector.tensor_reduce(row_sum[:], top8[:, :, 0:top], AX_X, ALU.add))
                link(nc.vector.reciprocal(row_inv[:], row_sum[:]))
                link(nc.vector.tensor_tensor(ex, pext[layer][:, :, 0:experts], prep[layer][:, :, 0:experts],
                                             ALU.subtract))
                weights = comb[:, :, COMB_COL[layer]:COMB_COL[layer] + experts]
                nc.vector.tensor_tensor(weights, ex, over(row_inv[:], experts), ALU.mult).then_inc(comb_ready, 1)
                if layer == 0:
                    dve.wait_ge(comb_ready, 1)
                    link(nc.vector.tensor_copy(comb_hi[:], weights))
                    for j in range(2):
                        nc.vector.tensor_copy(comb[:, :, j * E0:(j + 1) * E0], comb_hi[:].bitcast(F32)
                                              ).then_inc(comb_split, 1)
                    nc.vector.tensor_tensor(comb[:, :, 2 * E0:3 * E0], weights, comb_hi[:].bitcast(F32), ALU.subtract
                                            ).then_inc(comb_split, 1)

            def lower(half, step_no, hidden):
                dve.wait_ge(hi_done, step_no + 1)
                nc.vector.tensor_tensor(hid_lo[:, half, :], hidden, hid_hi[:, half, :].bitcast(F32),
                                        ALU.subtract).then_inc(lo_done, 1)

            def step(half, step_no, slot, loads):
                dve.wait_ge(act_done, step_no + 1 + CREDIT)
                if loads is not None:
                    dve.wait_ge(comb_in[slot], loads)
                nc.vector.tensor_tensor(ps_a[half][:], ps_a[half][:], comb_b[:, slot, half * HALF:(half + 1) * HALF],
                                        ALU.mult).then_inc(mult_done, 1)
                lower(half, step_no, ps_a[half][:])

            def shared_product(s):
                dve.wait_ge(act_done, BASE_SH + s + 1 + CREDIT)
                dve.wait_ge(linear_done, s + 1)
                nc.vector.tensor_tensor(shared_hid[:, s % 2, :], shared_banks(s)[1][:], shared_act[:, s % 2, :], ALU.mult
                                        ).then_inc(mult_done, 1)

            def shared_lower(s):
                lower(s % 2, BASE_SH + s, shared_hid[:, s % 2, :])

            def outputs(layer):
                for half in range(2):
                    dve.wait_ge(down_done, (STEPS0, LAST)[layer] - 1 + half + CREDIT)
                    nc.vector.tensor_scalar(y_t[:, 1, half * HALF:(half + 1) * HALF], ps_o[2 + half][:],
                                            tanh_g[:, 2 + layer:3 + layer], None, ALU.mult).then_inc(y_ready_dve, 1)

            def loaded(q):
                dve.wait_ge(x_in[q], 16)
                return None

            def add_read0(q):
                def invert_sum(p):
                    part = slice(2 * p, 2 * p + 2)
                    dve.wait_ge(probs_ready, 2 * p + 2)
                    gain_no[0] = mark(nc.vector.reciprocal(row_inv[:, part], row_sum[:, part]))

                def make_gain(p):
                    part = slice(2 * p, 2 * p + 2)
                    dve.wait_ge(vec, gain_no[0])
                    gain_no[0] = mark(nc.vector.scalar_tensor_tensor(
                        row_gain[:, part], row_inv[:, part], tanh_g[:, 0:1], valid[:, part], ALU.mult, ALU.mult))

                if q == 0:
                    invert_sum(0)
                    make_gain(0)
                if q == 1:
                    mask_scores(3)
                dve.wait_ge(read0_ready, q + 1)
                dve.wait_ge(vec, gain_no[0])
                for b in (2 * q, 2 * q + 1):
                    m = mark(nc.vector.scalar_tensor_tensor(xs[:, b, :], ps_t[q][:, (b % 2) * D:(b % 2 + 1) * D],
                                                            row_gain[:, b:b + 1], xs[:, b, :], ALU.mult, ALU.add))
                    if q < PAIRS - 1:
                        (invert_sum, make_gain)[b % 2](q + 1)
                return m

            def add_read1(b):
                dve.wait_ge(read1_ready, b + 1)
                return mark(nc.vector.scalar_tensor_tensor(xs[:, b, :], ps_r[b][:, 0:D],
                                                           tanh_g[:, 1:2], xs[:, b, :], ALU.mult, ALU.add))

            def add_output0(b):
                dve.wait_ge(y_turned, b // 2 + 1)
                return nc.vector.tensor_tensor(xs[:, b, :], ps_t[b // 2][:, (b % 2) * D:(b % 2 + 1) * D], xs[:, b, :],
                                               ALU.add)

            def add_output1(q):
                dve.wait_ge(y_turned, PAIRS + q + 1)
                pair = xs[:, 2 * q:2 * q + 2, :].rearrange("p b d -> p (b d)")
                return nc.vector.tensor_tensor(pair, ps_t[q][:], pair, ALU.add)

            nc.vector.memset(masked, NEG)
            nc.vector.memset(pext[0][:], -1.0)
            nc.vector.memset(pext[1][:], -1.0)
            link(nc.vector.memset(stats[:], 0.0))
            layernorm(0, loaded, lag=False)

            def norm(n, q):
                dve.wait_ge(rstd_ready, GROUPS_BEFORE[n] + q + 1)
                for b in (2 * q, 2 * q + 1):
                    nc.vector.tensor_scalar(xn[:, b, :], xs[:, b, :], mean_var[:, b, 0:1], rstd[:, b:b + 1],
                                            ALU.add, ALU.mult).then_inc(xn_ready_dve, 1)

            def mask_scores(q):
                part = slice(2 * q, 2 * q + 2)
                dve.wait_ge(score0_ready, q + 1)
                link(nc.vector.copy_predicated(masked[:, part, :], mask_sb[:, part, :],
                                               ps_o[q][:, 0:2 * S].rearrange("p (b s) -> p b s", b=2)))
                link(nc.vector.tensor_reduce(row_max[:, part], masked[:, part, :], AX_X, ALU.max))
                nc.vector.tensor_scalar(neg_max[:, part], row_max[:, part], -float(D) ** -0.5, None, ALU.mult
                                        ).then_inc(max_ready, 1)
                nc.vector.tensor_scalar(valid[:, part], row_max[:, part], NEG, None, ALU.is_gt)

            norm(0, 2)
            dve.wait_ge(mask_in, 16)
            mask_scores(0)
            norm(0, 3)
            mask_scores(1)
            mask_scores(2)
            dve.wait_ge(gains_ready, 1)
            dve.wait_ge(scale_ready, PAIRS)
            layernorm(1, add_read0, lag=True)
            norm(1, 3)
            take_turned(1, 2)
            lower_norm(1, 0)
            take_turned(1, 3)
            lower_norm(1, 1)
            shift(0, ps_o[2])
            probabilities(0)
            largest(0)
            take_out(0)
            combine(0)
            spread_first(0, ps_o[0])
            dve.wait_ge(first_spread_dve, 1)
            for s in range(2 * CH0):
                if s == 1:
                    dve.wait_ge(first_spread_act, 1)
                step(s % 2, s, s // 2 // SPAN0, 16 if s == 2 * SPAN0 else None)
            with dve.Fori(1, ROUNDS) as i:
                for s in range(2 * CH0):
                    slot = s // 2 // SPAN0
                    step(s % 2, i * (2 * CH0) + s, slot, i * 16 + 16 * slot if s % (2 * SPAN0) == 0 else None)
            outputs(0)
            dve.wait_ge(scale_ready, GROUPS_BEFORE[2])
            layernorm(2, lambda b: mark(add_output0(b)), lag=True)
            layernorm(3, add_read1, lag=False)
            take_turned(2, 2)
            lower_norm(2, 0)
            lower_norm(2, 1)
            take_turned(2, 3)
            shared_product(0)
            shift(1, ps_o[0])
            shared_lower(0)
            shared_product(1)
            shared_lower(1)
            probabilities(1)
            shared_product(2)
            largest(1)
            shared_lower(2)
            take_out(1)
            shared_product(3)
            shared_lower(3)
            combine(1)
            shared_product(4)
            shared_lower(4)
            spread_first(1, ps_a[0])
            shared_product(5)
            shared_lower(5)
            dve.wait_ge(first_spread_dve, 2)
            dve.wait_ge(first_spread_act, 2)
            with dve.Fori(0, ROUNDS) as i:
                for s in range(2 * CH1):
                    chunk, slot = s // 2, s // 2 % CSLOTS
                    layer0 = (ROUNDS - 2, ROUNDS, 0, 0)[slot]
                    loads = (i * (16 * spread_loads(slot, CH1)) + 16 * (layer0 + spread_loads(slot, chunk + 1))
                             if s % 2 == 0 else None)
                    step(s % 2, i * (2 * CH1) + (BASE1 + s), slot, loads)
            outputs(1)
            for q in range(PAIRS):
                add_output1(q).then_inc(out_ready, 1)


def kernel(**inputs):
    import numpy as np
    import concourse.bacc as bacc
    from concourse.bass_utils import run_bass_kernel_spmd

    a = {k: np.ascontiguousarray(v) for k, v in inputs.items()}

    def up_layout(rows):
        return rows.reshape(-1, P, KD, P).transpose(0, 3, 2, 1).reshape(-1, P, D)

    def padded(rows):
        return np.concatenate([rows, np.zeros((SHC * P - rows.shape[0], rows.shape[1]), rows.dtype)])

    gu = a["L1_ffn_shared_gate_up"]
    down = padded(a["L1_ffn_shared_down"].T).reshape(SHC, P, D)
    arrays = {
        "x": a["x"],
        "ctx": a["ctx_2048"],
        "ctx_t": a["ctx_2048"].reshape(B, S, KD, P).transpose(3, 0, 2, 1),
        "mask": a["mask_BxS2_bk0"],
        "g_xattn": a["g_xattn"],
        "g_ffn": a["g_ffn"],
        "gate0": a["L0_ffn_gate_w"].reshape(KD, P, E0).transpose(1, 0, 2),
        "gate0_b": a["L0_ffn_gate_b"],
        "w0": np.concatenate([up_layout(a["L0_ffn_w1"].transpose(0, 2, 1).reshape(E0 * F0, D)),
                              a["L0_ffn_w2"].reshape(-1, P, D)], axis=2),
        "b1": a["L0_ffn_b1"].reshape(-1, P).T,
        "b2": a["L0_ffn_b2"],
        "gate1": a["L1_ffn_gate_w"].reshape(E1, KD, P).transpose(2, 1, 0),
        "w1": np.concatenate([up_layout(a["L1_ffn_experts_w1"].reshape(E1 * I1, D)),
                              a["L1_ffn_experts_w2"].transpose(0, 2, 1).reshape(-1, P, D)], axis=2),
        "w_shared": np.concatenate([np.concatenate([up_layout(padded(gu[:SH1])), down], axis=2),
                                    np.concatenate([up_layout(padded(gu[SH1:])), np.zeros_like(down)], axis=2)]),
    }
    nc = bacc.Bacc("TRN2", target_bir_lowering=False, num_devices=1)
    args = {}
    for name, v in arrays.items():
        arrays[name] = v = np.ascontiguousarray(v)
        args[name] = nc.dram_tensor(f"in_{name}", v.shape, mybir.dt.from_np(v.dtype), kind="ExternalInput").ap()
    out = nc.dram_tensor("out_x", (B, S, D), F32, kind="ExternalOutput").ap()
    flamingo_kernel(nc, **args, out=out)
    r = run_bass_kernel_spmd(nc, [{f"in_{k}": v for k, v in arrays.items()}], core_ids=[0])
    return r.results[0]["out_x"]
```
